# Optimizing a Trainium2 kernel written in Bass

```python
import numpy as np
import jax
import jax.numpy as jnp

def _softmax(x, axis=-1):
    return jax.nn.softmax(x, axis=axis)

def _gelu(x):
    return jax.nn.gelu(x, approximate=True)

def _silu(x):
    return jax.nn.silu(x)

def _sigmoid(x):
    return jax.nn.sigmoid(x)

def _layernorm(x, axis=-1, eps=1e-05):
    m = jnp.mean(x, axis=axis, keepdims=True)
    v = jnp.var(x, axis=axis, keepdims=True)
    return (x - m) / jnp.sqrt(v + eps)

def _scatter_add(tgt, idx, src, axis=0):
    return tgt.at[idx].add(src)

def _segment_sum(src, seg, n):
    return jax.ops.segment_sum(src, seg, n)
kernel_name = 'mk_gnn_preln_d2_gnn_r8_cb760a'

def setup_inputs(seed: int=0):
    np.random.seed(seed)
    _w = jnp.asarray

    def _rec_inputs():
        import jax
        import jax.numpy as jnp
        _gk = jax.random.key(seed)
        x = -0.000202 + 1 * jax.random.normal(jax.random.fold_in(_gk, 1), (6250, 128), jnp.float32)
        _s = jax.random.randint(jax.random.fold_in(_gk, 2), (100000,), 0, 6250, jnp.int32)
        _d = jax.random.randint(jax.random.fold_in(_gk, 3), (100000,), 0, 6250, jnp.int32)
        _loop = jnp.arange(6250, dtype=jnp.int32)
        src = jnp.concatenate([_s, _d, _loop])
        dst = jnp.concatenate([_d, _s, _loop])
        _o = jnp.argsort(dst, stable=True)
        src = src[_o]
        dst = dst[_o]
        edge_attr_64 = jax.random.uniform(jax.random.fold_in(_gk, 11), (206250, 64), jnp.float32, 0.0, 1)
        return (x, src, dst, edge_attr_64)
    x, src, dst, edge_attr_64 = _rec_inputs()

    def _L0_gnn_setup():
        import jax, jax.numpy as jnp
        import numpy as np
        N_NODES = 6250
        key = jax.random.key(seed)
        k1, k2, k3, k4 = jax.random.split(key, 4)
        in_c, out_c = (128, 128)
        x = jax.random.normal(k1, (N_NODES, in_c), dtype=jnp.float32)
        edge_index = jax.random.randint(k2, (2, 75000), 0, N_NODES, dtype=jnp.int64)
        W_l = jax.random.normal(k3, (out_c, in_c), dtype=jnp.float32) / np.sqrt(in_c)
        W_r = jax.random.normal(k4, (out_c, in_c), dtype=jnp.float32) / np.sqrt(in_c)
        b = jnp.zeros((out_c,), dtype=jnp.float32)
        return {'x': x, 'edge_index': edge_index, 'W_l': W_l, 'W_r': W_r, 'b': b}
    _L0_gnn_all = _L0_gnn_setup()
    _L0_gnn_in = {k: v for k, v in _L0_gnn_all.items() if k in ('W_l', 'W_r', 'b')}
    del _L0_gnn_all

    def _L1_gnn_setup():
        import jax, jax.numpy as jnp
        import numpy as np
        N_NODES = 5000
        N_EDGES = 80000
        IN_CH = 128
        OUT_CH = 128
        NUM_RBF = 64
        key = jax.random.key(seed)
        ks = jax.random.split(key, 8)
        x = jax.random.normal(ks[0], (N_NODES, IN_CH), dtype=jnp.float32)
        edge_index = jax.random.randint(ks[1], (2, N_EDGES), 0, N_NODES, dtype=jnp.int64)
        edge_rbf = jax.random.uniform(ks[2], (N_EDGES, NUM_RBF), dtype=jnp.float32)
        s1 = 1.0 / np.sqrt(NUM_RBF)
        s2 = 1.0 / np.sqrt(OUT_CH)
        sl = 1.0 / np.sqrt(IN_CH)
        W1 = jax.random.normal(ks[3], (NUM_RBF, OUT_CH), dtype=jnp.float32) * s1
        b1 = jnp.zeros((OUT_CH,), dtype=jnp.float32)
        W2 = jax.random.normal(ks[4], (OUT_CH, OUT_CH), dtype=jnp.float32) * s2
        b2 = jnp.zeros((OUT_CH,), dtype=jnp.float32)
        Wl = jax.random.normal(ks[5], (IN_CH, OUT_CH), dtype=jnp.float32) * sl
        bl = jnp.zeros((OUT_CH,), dtype=jnp.float32)
        return {'x': x, 'edge_index': edge_index, 'edge_rbf': edge_rbf, 'W1': W1, 'b1': b1, 'W2': W2, 'b2': b2, 'Wl': Wl, 'bl': bl}
    _L1_gnn_all = _L1_gnn_setup()
    _L1_gnn_in = {k: v for k, v in _L1_gnn_all.items() if k in ('W1', 'b1', 'W2', 'b2', 'Wl', 'bl')}
    del _L1_gnn_all
    return {'x': x, 'src': src, 'dst': dst, 'edge_attr_64': edge_attr_64, 'L0_gnn_W_l': _L0_gnn_in['W_l'], 'L0_gnn_W_r': _L0_gnn_in['W_r'], 'L0_gnn_b': _L0_gnn_in['b'], 'L1_gnn_W1': _L1_gnn_in['W1'], 'L1_gnn_b1': _L1_gnn_in['b1'], 'L1_gnn_W2': _L1_gnn_in['W2'], 'L1_gnn_b2': _L1_gnn_in['b2'], 'L1_gnn_Wl': _L1_gnn_in['Wl'], 'L1_gnn_bl': _L1_gnn_in['bl']}

def reference(x, src, dst, edge_attr_64, L0_gnn_W_l, L0_gnn_W_r, L0_gnn_b, L1_gnn_W1, L1_gnn_b1, L1_gnn_W2, L1_gnn_b2, L1_gnn_Wl, L1_gnn_bl):
    import jax
    import jax.numpy as jnp

    def _L0_gnn_ref(x, edge_index, W_l, W_r, b):
        import jax, jax.numpy as jnp
        import numpy as np
        N_NODES = 6250
        src, dst = (edge_index[0], edge_index[1])
        msgs = x[src]
        summed = jax.ops.segment_sum(msgs, dst, num_segments=N_NODES)
        counts = jax.ops.segment_sum(jnp.ones_like(dst, dtype=x.dtype), dst, num_segments=N_NODES)
        agg = summed / jnp.maximum(counts, 1.0)[:, None]
        out = agg @ W_l.T + x @ W_r.T + b
        return jax.nn.log_softmax(out, axis=1)

    def _L1_gnn_ref(x, edge_index, edge_rbf, W1, b1, W2, b2, Wl, bl):
        import jax, jax.numpy as jnp
        import numpy as np
        N_NODES = 5000
        N_EDGES = 80000
        IN_CH = 128
        OUT_CH = 128
        NUM_RBF = 64
        weight = jnp.maximum(edge_rbf @ W1 + b1, 0.0) @ W2 + b2
        h = x @ Wl + bl
        row, col = (edge_index[0], edge_index[1])
        msg = h[col] * weight
        out = jax.ops.segment_sum(msg, row, num_segments=x.shape[0])
        return out
    edge_index = jnp.stack([src, dst])
    h = jnp.maximum(_layernorm(x, axis=-1), 0.0)
    x = x + _L0_gnn_ref(h, edge_index, L0_gnn_W_l, L0_gnn_W_r, L0_gnn_b)
    h = jnp.maximum(_layernorm(x, axis=-1), 0.0)
    x = x + _L1_gnn_ref(h, edge_index, edge_attr_64, L1_gnn_W1, L1_gnn_b1, L1_gnn_W2, L1_gnn_b2, L1_gnn_Wl, L1_gnn_bl)
    return x

_drawn_inputs = setup_inputs


def setup_inputs(seed=0):
    import zlib

    import numpy as np

    out = dict(_drawn_inputs(seed))
    spreads = {'L0_gnn_b': (0.0, 0.1),
     'L1_gnn_b1': (0.0, 0.1),
     'L1_gnn_b2': (0.0, 0.1),
     'L1_gnn_bl': (0.0, 0.1)}
    factors = {}
    for name, (base, spread) in spreads.items():
        noise = np.random.default_rng([zlib.crc32(name.encode()), seed]).standard_normal(out[name].shape)
        drawn = base * np.exp(spread * noise) if base else spread * noise
        out[name] = jnp.asarray(drawn.astype(out[name].dtype))
    for name, factor in factors.items():
        out[name] = (out[name] * factor).astype(out[name].dtype)
    return out
```

```python
import concourse.bass as bass
from concourse import mybir
from contextlib import ExitStack


def gnn_program(nc, x, src, dst, edge_attr, W_l, W_r, b_0, W1, b1, W2, b2, Wl, bl, out):
    fp32, bf16 = mybir.dt.float32, mybir.dt.bfloat16
    i32, i16 = mybir.dt.int32, mybir.dt.int16
    ALU = mybir.AluOpType
    ACT = mybir.ActivationFunctionType
    AX = mybir.AxisListType.X
    ds = bass.ds

    P = 128
    N, C = x.shape
    E, R = edge_attr.shape
    EPS = 1e-5
    NB = -(-N // P)
    NP = NB * P
    CB = 7
    NCH = NB // CB
    assert NCH * CB == NB and CB <= 8
    CW = CB * P
    NTAIL = N - (NB - 1) * P
    J = 4
    GE = J * P
    U = 4
    G = -(-E // GE)
    G += -G % U
    T = G * J
    TB = -(-T // P)
    TP = TB * P
    FULL_G = E // GE
    LAST_T = E - FULL_G * GE
    FULL_TB = E // (P * P)
    LAST_ROWS = (E - FULL_TB * P * P) // P
    LAST_COLS = E % P
    AGW = NP + P
    DUMP = NP
    ACCR = NP + P
    NACC = 4
    NO_NODE = 30000

    h0_d = nc.dram_tensor("h0_rows", (NP, C), fp32).ap()
    rows_d = nc.dram_tensor("edge_rows", (2, TP * P), i16).ap()
    acc_d = [nc.dram_tensor(f"acc{i}", (ACCR, C), fp32).ap() for i in range(NACC)]

    ctx = ExitStack()
    with ctx:
        def sb(name, shape, dt):
            return ctx.enter_context(nc.sbuf_tensor(name, shape, dt))

        def pb(name, shape, dt):
            return ctx.enter_context(nc.psum_tensor(name, shape, dt))

        def sem(name):
            return ctx.enter_context(nc.semaphore(name))

        X = sb("X", [P, NB, C], fp32)
        H = sb("H", [P, NB, C], fp32)
        E1 = sb("E1", [P, 2, CW], fp32)
        srccol = sb("srccol", [P, TP], fp32)
        dstloc = sb("dstloc", [P, TP], fp32)
        idx = sb("idx", [P, TP], i32)
        dup = sb("dup", [P, TP], fp32)
        rows = sb("rows", [P, U, 2, GE], i16)
        idxr = sb("idxr", [P, U, J], i32)
        ident = sb("ident", [P, P], fp32)
        iotaF = sb("iotaF", [P, P], fp32)
        iotaP = sb("iotaP", [P, 4], fp32)
        tri = sb("tri", [P, P], bf16)
        onesf = sb("onesf", [P, P], fp32)
        onesb = sb("onesb", [P, P], bf16)
        Wraw = sb("Wraw", [P, 2, C], fp32)
        WlrT = sb("WlrT", [P, 2, C], fp32)
        Wh = sb("Wh", [P, C], fp32)
        W1s = sb("W1s", [P, C], fp32)
        W2s = sb("W2s", [P, C], fp32)
        b1c = sb("b1c", [P, 1], fp32)
        brow = sb("brow", [1, 3, C], fp32)
        h0T = sb("h0T", [P, 2, CW], fp32)
        mean = sb("mean", [P, NB], fp32)
        var = sb("var", [P, NB], fp32)
        zmax = sb("zmax", [P, NB], fp32)
        zsum = sb("zsum", [P, NB], fp32)
        epsc = sb("epsc", [P, 1], fp32)

        big = sb("big", [P, 2 * AGW], fp32)
        agg = big[:, :].rearrange("p (a n) -> p a n", a=2)
        used = [0]

        def part(base, cursor, width):
            at = cursor[0]
            cursor[0] += width
            assert cursor[0] <= base.shape[1], (cursor, base.shape)
            return base[:, at:at + width]

        attr = part(big, used, U * J * R).rearrange("p (u f) -> p u f", u=U)
        attrT = part(big, used, 2 * 2 * P).rearrange("p (s q e) -> p s q e", s=2, q=2)
        hidT = part(big, used, 2 * GE).rearrange("p (s h q e) -> p s h q e", s=2, h=2, q=2)
        eqm = part(big, used, 2 * GE).rearrange("p (s j e) -> p s j e", s=2, j=J)
        hgs = part(big, used, 2 * GE).rearrange("p (s f) -> p s f", s=2)
        msg = part(big, used, 2 * GE).rearrange("p (s f) -> p s f", s=2)
        outr = part(big, used, U * GE).rearrange("p (u j c) -> p u j c", u=U, j=J)
        oht = part(big, used, 2 * GE).bitcast(bf16).rearrange("p (s w f) -> p s w f", s=2, w=2)

        par = sb("par", [P, (NB + 1) * 3 * C], bf16)
        h1p = par[:, :]
        parf = par[:, :].bitcast(fp32)
        ubs = [0]
        raw = part(parf, ubs, 2 * TP).bitcast(i32).rearrange("p (w b e) -> p w b e", w=2, b=TB)
        r16 = part(parf, ubs, TP).bitcast(i16).rearrange("p (w b e) -> p w b e", w=2, b=TB)
        Grow = part(parf, ubs, U * J * C).rearrange("p (u j c) -> p u j c", u=U, j=J)
        oh = part(parf, ubs, 2 * GE).rearrange("p (s j n) -> p s j n", s=2, j=J)
        rawf = H[:, :, :].rearrange("p b c -> p (b c)")[:, 0:2 * TP].rearrange("p (w b e) -> p w b e", w=2, b=TB)
        eqb = sb("eqb", [P, 2, 2, J, P], bf16)
        base_i = E1[:, :, :].rearrange("p a b -> p (a b)")[0:1, 0:TP].bitcast(i32)
        base_b = sb("base_b", [P, TB], i32)
        base_f = sb("base_f", [P, TB], fp32)
        off_i = dstloc[:, :].bitcast(i32)
        b2p = sb("b2p", [1, 3, C], bf16)
        b2r = sb("b2r", [1, 2, C], fp32)

        PS = pb("PS", [P, 8, 512], fp32)

        psA = PS[:, 0:4, :].rearrange("p b f -> p (b f)").rearrange("p (s j a n) -> p s j a n", s=2, j=J, a=2)
        psD = PS[:, 4:6, 0:J]
        psZ = PS[:, 0:4, :].rearrange("p (s b) f -> p s (b f)", s=2)
        psT = PS[:, 4:8, :].rearrange("p (s b) f -> p s (b f)", s=2)
        pTP = PS[:, 0, 0:2 * P].rearrange("p (q e) -> p q e", q=2)
        pHID = PS[:, 1:3, 0:2 * P]
        pW = PS[:, 3:5, :]
        pHG = PS[:, 5, :]
        pDD = PS[:, 6:8, :]

        names = """x_in raw_in w_in consts cast_done colT_done srccol_ready dstcol_ready bcast_done tables_ready
            rows16_ready rows_out zero_ready acc0_x dump_zero h0_ready h0_out sq_done sq1 std_ready std1 wT_done wT_ready
            idx_ready sums_done oh_ready eq_ready dups_done dup_copied agg_done eqtri_done
            aggn_ready hT_done hT_copied z_done zs_ready exp_done sum_ready ln_done x1_ready
            h1a_ready hiT mid_ready h1_ready off_ready tail_in d_consts b2_ready
            tp_done attrT_ready hid_done relu_done w_done hg_done hgc_done oht_ready eqm_ready msg_done dd_done
            out_ready fin_in0 fin_in1 fin_done out_done0 out_done1 chain pool_c lnT lnT_copied hw_done hw_copied adj_ready""".split()
        S = {n: sem(n) for n in names}
        S_gat = [[sem(f"gathered_{k}_{j}") for j in range(J)] for k in range(U)]
        S_srow = [sem(f"src_row_in_{k}") for k in range(U)]
        S_rows = [sem(f"rows_in_{k}") for k in range(U)]
        S_attr = [sem(f"attr_in_{k}") for k in range(U)]
        S_acc = [sem(f"acc_added_{a}") for a in range(NACC)]
        S_zero = sem("acc_zeroed")

        def wait(eng, s, v):
            if not (isinstance(v, int) and v <= 0):
                eng.wait_ge(s, v)

        def landed(s, k):
            return 4 * (s - k) + 16

        assert U == 4

        def steps(eng, step):
            for s in range(U):
                step(s, s)
            with eng.Fori(1, G // U - 1) as i:
                for k in range(U):
                    step(i * U + k, k)
            for s in range(G - U, G):
                step(s, s % U)

        def chunk(c):
            return slice(c * CB, (c + 1) * CB)

        FP = 125
        FN, FB = N // FP, 10
        FW = FB * C
        fin = big[0:FP, 0:2 * NACC * FW].rearrange("p (s a f) -> p s a f", s=2, a=NACC)
        fino = X[:, :, :].rearrange("p b c -> p (b c)")[0:FP, 0:2 * FW].rearrange("p (s f) -> p s f", s=2)
        less_dump = E1[:, :, :].rearrange("p a b -> p (a b)")
        assert TP <= 2 * CW
        NTR = -(-TB // 4)

        block = ctx.enter_context(nc.Block())

        @block.sync
        def _(sp):
            sp.wait_ge(S["zero_ready"], 1)
            for c in range(NCH):
                lo, hi = c * CB, min((c + 1) * CB, NB - 1)
                sp.dma_start(X[:, lo:hi, :], x[lo * P:hi * P, :].rearrange("(b p) c -> p b c", p=P)).then_inc(S["x_in"], 16)
                if c == NCH - 1:
                    sp.dma_start(X[0:NTAIL, NB - 1, :], x[(NB - 1) * P:N, :]).then_inc(S["tail_in"], 16)
                sp.wait_ge(S["x_in"], 16 * (c + 1))
            sp.dma_start(W1s[0:R, :], W1).then_inc(S["w_in"], 16)
            sp.dma_start(W1s[R:2 * R, :], W1).then_inc(S["w_in"], 16)
            sp.dma_start(W2s[:, :], W2).then_inc(S["w_in"], 16)
            sp.dma_start(Wraw[:, 0, :], W_l).then_inc(S["w_in"], 16)
            sp.dma_start(Wraw[:, 1, :], W_r).then_inc(S["w_in"], 16)
            sp.dma_start(Wh[:, :], Wl).then_inc(S["w_in"], 16)
            sp.dma_start(b1c[:, :], b1.rearrange("(p a) -> p a", a=1)).then_inc(S["w_in"], 16)
            for n, v in enumerate((b_0, bl, b2)):
                sp.dma_start(brow[:, n, :], v.rearrange("(a c) -> a c", a=1)).then_inc(S["w_in"], 16)
            for c in range(NCH):
                sp.wait_ge(S["h0_ready"], c + 1)
                sp.dma_start(h0_d[c * CW:(c + 1) * CW, :].rearrange("(b p) c -> p b c", p=P),
                             H[:, chunk(c), :]).then_inc(S["h0_out"], 16)
            sp.wait_ge(S["rows16_ready"], 1)
            for w in range(2):
                sp.dma_start(rows_d[w, :].rearrange("(b p e) -> p b e", p=P, e=P), r16[:, w, :, :]).then_inc(S["rows_out"], 16)
            sp.wait_ge(S["rows_out"], 32)

            def src_row(g, k):
                wait(sp, S["eq_ready"], g - U + 1)
                sp.dma_start(rows[:, k, 1, :], rows_d[1, ds(g * GE, GE)].partition_broadcast(P)).then_inc(S_srow[k], 16)

            steps(sp, src_row)

            for c in range(NCH):
                sp.wait_ge(S["x1_ready"], c + 1)
                hi = min((c + 1) * CB, NB - 1)
                sp.dma_start(acc_d[0][c * CW:hi * P, :].rearrange("(b p) c -> p b c", p=P),
                             X[:, c * CB:hi, :]).then_inc(S["acc0_x"], 16)
            sp.dma_start(acc_d[0][hi * P:N, :], X[0:NTAIL, NB - 1, :]).then_inc(S["acc0_x"], 16)

            def edge_loads(g, k):
                wait(sp, S["eqm_ready"], g - U + 1)
                wait(sp, S["oht_ready"], g - U + 1)
                sp.dma_start(rows[:, k, :, :], rows_d[:, ds(g * GE, GE)].partition_broadcast(P)).then_inc(S_rows[k], 16)
                wait(sp, S["tp_done"], g - U + 1)
                if not isinstance(g, int) or g < FULL_G:
                    sp.dma_start(attr[:, k, :].rearrange("p (j f) -> p j f", j=J),
                                 edge_attr[ds(g * GE, GE), :].rearrange("(j p) f -> p j f", p=P)).then_inc(S_attr[k], 16)
                elif g == FULL_G:
                    full = LAST_T // P
                    sp.dma_start(attr[:, k, 0:full * R].rearrange("p (j f) -> p j f", j=full),
                                 edge_attr[g * GE:g * GE + full * P, :].rearrange("(j p) f -> p j f", p=P)).then_inc(S_attr[k], 16)
                    sp.dma_start(attr[0:LAST_T - full * P, k, full * R:(full + 1) * R],
                                 edge_attr[g * GE + full * P:E, :]).then_inc(S_attr[k], 16)

            sp.wait_ge(S["h1_ready"], 1)
            steps(sp, edge_loads)
            for a in range(NACC):
                sp.wait_ge(S_acc[a], 16 * G)
            for c in range(FN // FB):
                if c >= 2:
                    sp.wait_ge(S["fin_done"], c - 1)
                for a in range(NACC):
                    sp.dma_start(fin[:, c % 2, a, :], acc_d[a][0:N, :].rearrange("(p b) c -> p (b c)", p=FP)
                                 [:, c * FB * C:(c + 1) * FB * C]).then_inc(S[f"fin_in{c % 2}"], 16)
                if c >= 1:
                    sp.wait_ge(S["fin_done"], c)
                    sp.dma_start(out.rearrange("(p b) c -> p (b c)", p=FP)[:, (c - 1) * FB * C:c * FB * C],
                                 fino[:, (c - 1) % 2, :]).then_inc(S[f"out_done{(c - 1) % 2}"], 16)
            last = FN // FB - 1
            sp.wait_ge(S["fin_done"], last + 1)
            sp.dma_start(out.rearrange("(p b) c -> p (b c)", p=FP)[:, last * FB * C:(last + 1) * FB * C],
                         fino[:, last % 2, :]).then_inc(S[f"out_done{last % 2}"], 16)
            for c in range(2):
                sp.wait_ge(S[f"out_done{c}"], 16 * ((last + 2 - c) // 2))

        @block.gpsimd
        def _(pool):
            pool.memset(X[:, NB - 1, :], 0.0).then_inc(S["zero_ready"], 1)
            pool.memset(raw[:, 0, TB - 1, :], NO_NODE).then_inc(S["pool_c"], 1)
            pool.memset(raw[:, 1, TB - 1, :], N).then_inc(S["pool_c"], 1)
            pool.wait_ge(S["pool_c"], 2)
            for w, v in enumerate((dst, src)):
                pool.dma_start(raw[:, w, 0:FULL_TB, :], v[0:FULL_TB * P * P].rearrange("(b p e) -> p b e", p=P, e=P)).then_inc(S["raw_in"], 16)
                at = FULL_TB * P * P
                pool.dma_start(raw[0:LAST_ROWS, w, FULL_TB, :], v[at:at + LAST_ROWS * P].rearrange("(p e) -> p e", e=P)).then_inc(S["raw_in"], 16)
                at += LAST_ROWS * P
                pool.dma_start(raw[LAST_ROWS:LAST_ROWS + 1, w, FULL_TB, 0:LAST_COLS],
                               v[at:E].rearrange("(a e) -> a e", a=1)).then_inc(S["raw_in"], 16)
            pool.iota(iotaF[:, :], pattern=[[1, P]], base=0, channel_multiplier=0, allow_small_or_imprecise_dtypes=True).then_inc(S["consts"], 1)
            pool.iota(iotaP[:, 0:2], pattern=[[P, 2]], base=0, channel_multiplier=1, allow_small_or_imprecise_dtypes=True).then_inc(S["consts"], 1)
            pool.iota(iotaP[:, 2:3], pattern=[[1, 1]], base=DUMP, channel_multiplier=1, allow_small_or_imprecise_dtypes=True).then_inc(S["consts"], 1)
            pool.memset(onesf[:, :], 1.0).then_inc(S["consts"], 1)
            pool.memset(onesb[:, :], 1.0).then_inc(S["consts"], 1)
            pool.memset(epsc[:, :], EPS).then_inc(S["consts"], 1)
            pool.memset(big[:, :], 0.0).then_inc(S["consts"], 1)
            pool.wait_ge(S["consts"], 7)
            for a in range(NACC):
                if a:
                    pool.dma_start(acc_d[a].rearrange("(p b) c -> p (b c)", p=P), big[:, 0:ACCR // P * C]).then_inc(S_zero, 16)
                else:
                    pool.dma_start(acc_d[0][N:NP, :], big[0:NP - N, 0:C]).then_inc(S_zero, 16)
                    pool.dma_start(acc_d[0][NP:ACCR, :], big[:, 0:C]).then_inc(S_zero, 16)
            pool.wait_ge(S_zero, 16 * (NACC + 1))
            pool.nop().then_inc(S["dump_zero"], 1)

            filled, freed = pool.alloc_register("filled"), pool.alloc_register("freed")
            added = [pool.alloc_register(f"added{j}") for j in range(J)]
            pool.reg_mov(filled, U + 1)
            pool.reg_mov(freed, 1)

            pool.wait_ge(S["h0_out"], 16 * NCH)

            def gather(g, k):
                if isinstance(g, int):
                    pool.wait_ge(S["idx_ready"], g + 1)
                    wait(pool, S["sums_done"], g - U + 1)
                else:
                    pool.wait_ge(S["idx_ready"], filled)
                    pool.reg_add(filled, filled, 1)
                    pool.wait_ge(S["sums_done"], freed)
                    pool.reg_add(freed, freed, 1)
                for j in range(J):
                    pool.indirect_dma_start(Grow[:, k, j, :], None, h0_d,
                                            bass.IndirectOffsetOnAxis(ap=idxr[:, k, j:j + 1], axis=0)).then_inc(S_gat[k][j], 16)

            steps(pool, gather)
            pool.wait_ge(S["acc0_x"], 16 * (NCH + 1))

            pool.reg_mov(filled, U + 1)
            for r in added:
                pool.reg_mov(r, 16 * U)

            def scatter(g, k):
                if isinstance(g, int):
                    pool.wait_ge(S["out_ready"], g + 1)
                else:
                    pool.wait_ge(S["out_ready"], filled)
                    pool.reg_add(filled, filled, 1)
                for j in range(J):
                    if isinstance(g, int):
                        wait(pool, S_acc[j], 16 * g)
                    else:
                        pool.wait_ge(S_acc[j], added[j])
                        pool.reg_add(added[j], added[j], 16)
                    pool.indirect_dma_start(acc_d[j], bass.IndirectOffsetOnAxis(ap=idxr[:, k, j:j + 1], axis=0),
                                            outr[:, k, j, :], None, compute_op=ALU.add).then_inc(S_acc[j], 16)

            steps(pool, scatter)

        def dve_link(eng):
            count = [0]

            def link(ins):
                count[0] += 1
                ins.then_inc(S["chain"], 1)
                eng.wait_ge(S["chain"], count[0])
            return link

        @block.vector
        def _(dve):
            link = dve_link(dve)

            def bc(col):
                return col.unsqueeze(2).to_broadcast([P, CB, P])

            dve.wait_ge(S["consts"], 7)
            nc.vector.tensor_scalar(ident[:, :], iotaF[:, :], iotaP[:, 0:1], None, ALU.is_equal).then_inc(S["d_consts"], 1)
            nc.vector.tensor_scalar(tri[:, :], iotaF[:, :], iotaP[:, 0:1], None, ALU.is_gt).then_inc(S["d_consts"], 1)

            dve.wait_ge(S["raw_in"], 96)
            nc.vector.tensor_copy(rawf[:, 0, :, :], raw[:, 0, :, :]).then_inc(S["cast_done"], 1)
            nc.vector.tensor_copy(rawf[:, 1, :, :], raw[:, 1, :, :]).then_inc(S["cast_done"], 1)
            nc.vector.tensor_copy(r16[:, 1, :, :], raw[:, 1, :, :])
            link(nc.vector.tensor_scalar(base_b[:, :], raw[:, 0, :, 0], -P, None, ALU.bitwise_and))
            link(nc.vector.tensor_copy(base_f[:, :], base_b[:, :]))
            dve.wait_ge(S["cast_done"], 2)
            nc.vector.tensor_tensor(r16[:, 0, :, :], rawf[:, 0, :, :], base_f[:, :].unsqueeze(2).to_broadcast([P, TB, P]),
                                    ALU.subtract).then_inc(S["rows16_ready"], 1)
            for n in range(2 * NTR):
                w, q = divmod(n, NTR)
                blocks = min(4, TB - 4 * q)
                dve.wait_ge(S["colT_done"], n + 1)
                ps = psT[:, n % 2, 0:blocks * P]
                to = (dstloc, srccol)[w][:, 4 * q * P:4 * q * P + blocks * P]
                nc.vector.tensor_copy(to, ps).then_inc(S["dstcol_ready" if w == 0 else "srccol_ready"], 1)
            dve.wait_ge(S["srccol_ready"], NTR)
            nc.vector.tensor_copy(idx[:, :], srccol[:, :]).then_inc(S["tables_ready"], 1)

            def norm_mean(c):
                link(nc.vector.tensor_reduce(mean[:, chunk(c)], X[:, chunk(c), :], AX, ALU.add))
                link(nc.vector.tensor_scalar(mean[:, chunk(c)], mean[:, chunk(c)], 1.0 / C, None, ALU.mult))
                nc.vector.tensor_tensor(H[:, chunk(c), :], X[:, chunk(c), :], bc(mean[:, chunk(c)]), ALU.subtract)\
                    .then_inc(S["lnT"], 1)

            def norm_scale(c, n):
                dve.wait_ge(S["sq_done"], n + 1)
                link(nc.vector.tensor_reduce(var[:, chunk(c)], E1[:, n % 2, :].rearrange("p (b c) -> p b c", c=C), AX, ALU.add))
                nc.vector.tensor_scalar(var[:, chunk(c)], var[:, chunk(c)], 1.0 / C, None, ALU.mult).then_inc(S["lnT_copied"], 1)
                dve.wait_ge(S["std_ready"], n + 1)
                link(nc.vector.reciprocal(var[:, chunk(c)], var[:, chunk(c)]))

            dve.wait_ge(S["colT_done"], 2 * NTR)
            for c in range(NCH + 1):
                if c < NCH:
                    dve.wait_ge(S["x_in"], 16 * (c + 1))
                    if c == NCH - 1:
                        dve.wait_ge(S["tail_in"], 16)
                    norm_mean(c)
                if c:
                    norm_scale(c - 1, c - 1)
                    nc.vector.scalar_tensor_tensor(out=H[:, chunk(c - 1), :], in0=H[:, chunk(c - 1), :], scalar=0.0,
                                                   in1=bc(var[:, chunk(c - 1)]), op0=ALU.max, op1=ALU.mult).then_inc(S["h0_ready"], 1)

            link(nc.vector.tensor_copy(base_i, dstloc[0:1, :]))
            link(nc.vector.memset(base_i[:, T - (T - -(-E // P)):TP], 0))
            for q in range(NTR):
                w = min(512, TP - q * 512)
                dve.wait_ge(S["bcast_done"], q + 1)
                link(nc.vector.tensor_tensor(dstloc[:, q * 512:q * 512 + w], dstloc[:, q * 512:q * 512 + w],
                                             psZ[:, q // 2, (q % 2) * 512:(q % 2) * 512 + w], ALU.subtract))
            link(nc.vector.memset(dstloc[:, -(-E // P):TP], float(NO_NODE)))

            dve.wait_ge(S["wT_done"], 1)
            nc.vector.tensor_copy(WlrT[:, :, :], psT[:, 0, 0:2 * C].rearrange("p (w c) -> p w c", w=2)).then_inc(S["wT_ready"], 1)
            dve.wait_ge(S["w_in"], 160)
            link(nc.vector.tensor_copy(b2p[:, 0, :], brow[:, 2, :]))
            link(nc.vector.tensor_tensor(b2r[:, 0, :], brow[:, 2, :], b2p[:, 0, :], ALU.subtract))
            link(nc.vector.tensor_copy(b2p[:, 1, :], b2r[:, 0, :]))
            link(nc.vector.tensor_tensor(b2p[:, 2, :], b2r[:, 0, :], b2p[:, 1, :], ALU.subtract))
            dve.wait_ge(S["dump_zero"], 1)

            def idx_columns(g, k):
                nc.vector.tensor_copy(idxr[:, k, :], idx[:, ds(g * J, J)]).then_inc(S["idx_ready"], 1)

            def one_hot(g, k):
                wait(dve, S["sums_done"], g - 1)
                nc.vector.tensor_tensor(oh[:, k % 2, :, :], iotaF[:, :].unsqueeze(1).to_broadcast([P, J, P]),
                                        dstloc[:, ds(g * J, J)].unsqueeze(2).to_broadcast([P, J, P]), ALU.is_equal)\
                    .then_inc(S["oh_ready"], 1)

            def equals(g, k):
                dve.wait_ge(S_srow[k], landed(g, k))
                nc.vector.tensor_tensor(eqb[:, k % 2, 0, :, :], rows[:, k, 1, :].rearrange("p (j e) -> p j e", j=J),
                                        srccol[:, ds(g * J, J)].unsqueeze(2).to_broadcast([P, J, P]), ALU.is_equal)\
                    .then_inc(S["eq_ready"], 1)
                dve.wait_ge(S["eq_ready"], g + 1)
                wait(dve, S["dups_done"], g - 1)
                nc.vector.tensor_tensor(eqb[:, k % 2, 1, :, :], eqb[:, k % 2, 0, :, :],
                                        tri[:, :].unsqueeze(1).to_broadcast([P, J, P]), ALU.mult).then_inc(S["eqtri_done"], 1)

            base_regs = [dve.alloc_register(f"base{j}") for j in range(J)]

            def add_sums(g, k):
                dve.load(base_regs, base_i[0:1, ds(g * J, J)])
                first = [dve.snap(r, min_val=0, max_val=NP) for r in base_regs]
                dve.wait_ge(S["sums_done"], g + 1)
                for j, at in enumerate(first):
                    wait(dve, S["agg_done"], g * J + j)
                    nc.vector.tensor_tensor(agg[:, :, ds(at, P)], agg[:, :, ds(at, P)], psA[:, k % 2, j, :, :], ALU.add)\
                        .then_inc(S["agg_done"], 1)

            def dup_counts(g, k):
                dve.wait_ge(S["dups_done"], g + 1)
                nc.vector.tensor_copy(dup[:, ds(g * J, J)], psD[:, k % 2, :]).then_inc(S["dup_copied"], 1)

            for g in range(U):
                idx_columns(g, g)
            one_hot(0, 0)
            equals(0, 0)

            def layer0(s, k, ahead=True, more=True):
                if ahead:
                    one_hot(s + 1, (k + 1) % U)
                    equals(s + 1, (k + 1) % U)
                add_sums(s, k)
                dup_counts(s, k)
                if more:
                    idx_columns(s + U, k)

            for s in range(U):
                layer0(s, s)
            with dve.Fori(1, G // U - 1) as i:
                for k in range(U):
                    layer0(i * U + k, k)
            for s in range(G - U, G):
                layer0(s, s % U, s + 1 < G, False)

            dve.wait_ge(S["agg_done"], T)
            dve.wait_ge(S["dup_copied"], G)
            link(nc.vector.tensor_scalar(off_i[0:1, 0:TP], base_i, -P, None, ALU.bitwise_and))
            link(nc.vector.tensor_scalar(off_i[0:1, 0:TP], off_i[0:1, 0:TP], float(3 * C // P), None, ALU.mult))
            link(nc.vector.tensor_scalar(dup[:, 0:T], dup[:, 0:T], 1.0, None, ALU.min))
            link(nc.vector.scalar_tensor_tensor(out=less_dump[:, 0:T], in0=srccol[:, 0:T], scalar=iotaP[:, 2:3], in1=dup[:, 0:T],
                                                op0=ALU.subtract, op1=ALU.mult))
            link(nc.vector.tensor_tensor(idx[:, 0:T], srccol[:, 0:T], less_dump[:, 0:T], ALU.subtract))
            for g in range(U):
                nc.vector.tensor_copy(idxr[:, g, :], idx[:, g * J:(g + 1) * J]).then_inc(S["adj_ready"], 1)

            def means(c):
                w = slice(c * CW, (c + 1) * CW)
                link(nc.vector.tensor_scalar(agg[:, 1, w], agg[:, 1, w], 1.0, None, ALU.max))
                link(nc.vector.reciprocal(agg[:, 1, w], agg[:, 1, w]))
                nc.vector.tensor_tensor(agg[:, 0, w], agg[:, 0, w], agg[:, 1, w], ALU.mult).then_inc(S["aggn_ready"], 1)

            def z3(c):
                return psZ[:, c % 2, 0:CW].rearrange("p (b c) -> p b c", c=C)

            def logits(c):
                dve.wait_ge(S["z_done"], c + 1)
                link(nc.vector.tensor_reduce(zmax[:, chunk(c)], z3(c), AX, ALU.max))
                nc.vector.tensor_tensor(H[:, chunk(c), :], z3(c), bc(zmax[:, chunk(c)]), ALU.subtract).then_inc(S["zs_ready"], 1)

            def softmax_sum(c):
                dve.wait_ge(S["exp_done"], c + 1)
                nc.vector.tensor_reduce(zsum[:, chunk(c)], E1[:, c % 2, :].rearrange("p (b c) -> p b c", c=C), AX, ALU.add)\
                    .then_inc(S["sum_ready"], 1)

            def add_to_x(c):
                dve.wait_ge(S["ln_done"], c + 1)
                link(nc.vector.tensor_tensor(H[:, chunk(c), :], H[:, chunk(c), :], bc(zsum[:, chunk(c)]), ALU.subtract))
                nc.vector.tensor_tensor(X[:, chunk(c), :], X[:, chunk(c), :], H[:, chunk(c), :], ALU.add).then_inc(S["x1_ready"], 1)
                dve.wait_ge(S["x1_ready"], c + 1)

            for c in range(NCH):
                means(c)
            for c in range(NCH + 1):
                if c < NCH:
                    logits(c)
                if c:
                    softmax_sum(c - 1)
                    add_to_x(c - 1)
            for c in range(NCH + 1):
                if c < NCH:
                    norm_mean(c)
                if c:
                    norm_scale(c - 1, NCH + c - 1)
                    nc.vector.scalar_tensor_tensor(out=H[:, chunk(c - 1), :], in0=H[:, chunk(c - 1), :], scalar=0.0,
                                                   in1=bc(var[:, chunk(c - 1)]), op0=ALU.max, op1=ALU.mult).then_inc(S["h1a_ready"], 1)
            hp = h1p.rearrange("p (b a c) -> p b a c", a=3, c=C)
            nc.vector.memset(hp[:, NB, :, :], 0.0).then_inc(S["mid_ready"], 1)
            for c in range(NCH):
                dve.wait_ge(S["hiT"], c + 1)
                full = z3(c)
                r = H[:, chunk(c), :]
                link(nc.vector.tensor_copy(hp[:, chunk(c), 0, :], full))
                link(nc.vector.tensor_tensor(r, full, hp[:, chunk(c), 0, :], ALU.subtract))
                link(nc.vector.tensor_copy(hp[:, chunk(c), 1, :], r))
                nc.vector.tensor_tensor(hp[:, chunk(c), 2, :], r, hp[:, chunk(c), 1, :], ALU.subtract).then_inc(S["mid_ready"], 1)
            dve.wait_ge(S["mid_ready"], NCH + 1)
            nc.vector.memset(attr, 0.0).then_inc(S["h1_ready"], 1)

            def one_hot_T(g, k):
                dve.wait_ge(S_rows[k], landed(g, k))
                wait(dve, S["hg_done"], g - 1)
                for w in range(2):
                    last = nc.vector.tensor_scalar(oht[:, k % 2, w, :], rows[:, k, 0, :], iotaP[:, w:w + 1], None, ALU.is_equal)
                last.then_inc(S["oht_ready"], 1)

            def equality(g, k):
                wait(dve, S["dd_done"], g - 1)
                nc.vector.tensor_tensor(eqm[:, k % 2, :, :], rows[:, k, 1, :].rearrange("p (j e) -> p j e", j=J),
                                        srccol[:, ds(g * J, J)].unsqueeze(2).to_broadcast([P, J, P]), ALU.is_equal)\
                    .then_inc(S["eqm_ready"], 1)

            def messages(g, k):
                dve.wait_ge(S["w_done"], g + 1)
                dve.wait_ge(S["hgc_done"], g + 1)
                wait(dve, S["dd_done"], g - 1)
                nc.vector.tensor_tensor(msg[:, k % 2, :], pW[:, k % 2, :], hgs[:, k % 2, :], ALU.mult).then_inc(S["msg_done"], 1)

            def sums_out(g, k):
                dve.wait_ge(S["dd_done"], g + 1)
                for j in range(J):
                    wait(dve, S_acc[j], 16 * (g - U + 1))
                nc.vector.tensor_copy(idxr[:, k, :], idx[:, ds(g * J, J)])
                nc.vector.tensor_copy(outr[:, k, :, :], pDD[:, k % 2, :].rearrange("p (j c) -> p j c", j=J)).then_inc(S["out_ready"], 1)

            one_hot_T(0, 0)
            equality(0, 0)

            def layer1(s, k):
                if not isinstance(s, int) or s + 1 < G:
                    one_hot_T(s + 1, (k + 1) % U)
                    equality(s + 1, (k + 1) % U)
                messages(s, k)
                if not isinstance(s, int) or s > 0:
                    sums_out(s - 1, (k - 1) % U)

            steps(dve, layer1)
            sums_out(G - 1, (G - 1) % U)

            for c in range(FN // FB):
                dve.wait_ge(S[f"fin_in{c % 2}"], 64 * (c // 2 + 1))
                link(nc.vector.tensor_tensor(fin[:, c % 2, 0, :], fin[:, c % 2, 0, :], fin[:, c % 2, 1, :], ALU.add))
                link(nc.vector.tensor_tensor(fin[:, c % 2, 2, :], fin[:, c % 2, 2, :], fin[:, c % 2, 3, :], ALU.add))
                if c >= 2:
                    dve.wait_ge(S[f"out_done{c % 2}"], 16 * (c // 2))
                nc.vector.tensor_tensor(fino[:, c % 2, :], fin[:, c % 2, 0, :], fin[:, c % 2, 2, :], ALU.add).then_inc(S["fin_done"], 1)

        @block.tensor
        def _(pe):
            pe.wait_ge(S["d_consts"], 2)
            pe.wait_ge(S["cast_done"], 2)
            for n in range(2 * NTR):
                w, q = divmod(n, NTR)
                wait(pe, S["dstcol_ready"], min(n - 1, NTR))
                wait(pe, S["srccol_ready"], n - 1 - NTR)
                for i in range(min(4, TB - 4 * q)):
                    last = nc.tensor.transpose(psT[:, n % 2, i * P:(i + 1) * P], rawf[:, w, 4 * q + i, :], ident[:, :])
                last.then_inc(S["colT_done"], 1)
            pe.wait_ge(S["dstcol_ready"], NTR)
            for q in range(NTR):
                w = min(512, TP - q * 512)
                nc.tensor.matmul(psZ[:, q // 2, (q % 2) * 512:(q % 2) * 512 + w], onesf[0:1, :], dstloc[0:1, q * 512:q * 512 + w],
                                 start=True, stop=True).then_inc(S["bcast_done"], 1)
            pe.wait_ge(S["srccol_ready"], NTR)
            pe.wait_ge(S["w_in"], 160)
            for w in range(2):
                last = nc.tensor.transpose(psT[:, 0, w * C:(w + 1) * C], Wraw[:, w, :], ident[:, :])
            last.then_inc(S["wT_done"], 1)
            pe.wait_ge(S["wT_ready"], 1)

            def layer0(g, k):
                pe.wait_ge(S["oh_ready"], g + 1)
                wait(pe, S["agg_done"], J * (g - 1))
                for j in range(J):
                    pe.wait_ge(S_gat[k][j], landed(g, k))
                    nc.tensor.matmul(psA[:, k % 2, j, 0, :], Grow[:, k, j, :], oh[:, k % 2, j, :], start=True, stop=True)
                    last = nc.tensor.matmul(psA[:, k % 2, j, 1, :], onesf[:, :], oh[:, k % 2, j, :], start=True, stop=True)
                last.then_inc(S["sums_done"], 1)
                pe.wait_ge(S["eqtri_done"], g + 1)
                wait(pe, S["dup_copied"], g - 1)
                for j in range(J):
                    last = nc.tensor.matmul(psD[:, k % 2, j:j + 1], eqb[:, k % 2, 1, j, :], onesb[:, 0:1], start=True, stop=True)
                last.then_inc(S["dups_done"], 1)

            steps(pe, layer0)

            def transposes(c, n):
                wait(pe, S["hT_copied"], n - 1)
                for i in range(CB):
                    last = nc.tensor.transpose(psT[:, n % 2, i * P:(i + 1) * P], H[:, c * CB + i, :], ident[:, :])
                last.then_inc(S["hT_done"], 1)

            pe.wait_ge(S["dup_copied"], G)
            transposes(0, 0)
            for c in range(NCH):
                if c + 1 < NCH:
                    transposes(c + 1, c + 1)
                pe.wait_ge(S["aggn_ready"], c + 1)
                pe.wait_ge(S["hT_copied"], c + 1)
                wait(pe, S["zs_ready"], c - 1)
                for i in range(CB):
                    z = psZ[:, c % 2, i * P:(i + 1) * P]
                    n0 = (c * CB + i) * P
                    nc.tensor.matmul(z, agg[:, 0, n0:n0 + P], WlrT[:, 0, :], start=True, stop=False)
                    nc.tensor.matmul(z, h0T[:, c % 2, i * P:(i + 1) * P], WlrT[:, 1, :], start=False, stop=False)
                    last = nc.tensor.matmul(z, onesf[0:1, :], brow[0:1, 0, :], start=False, stop=True)
                last.then_inc(S["z_done"], 1)
            pe.wait_ge(S["zs_ready"], NCH)
            for c in range(NCH):
                pe.wait_ge(S["h1a_ready"], c + 1)
                transposes(c, NCH + c)
                pe.wait_ge(S["hT_copied"], NCH + c + 1)
                wait(pe, S["mid_ready"], c)
                for i in range(CB):
                    z = psZ[:, c % 2, i * P:(i + 1) * P]
                    nc.tensor.matmul(z, h0T[:, (NCH + c) % 2, i * P:(i + 1) * P], Wh[:, :], start=True, stop=False)
                    last = nc.tensor.matmul(z, onesf[0:1, :], brow[0:1, 1, :], start=False, stop=True)
                last.then_inc(S["hiT"], 1)

            pe.wait_ge(S["h1_ready"], 1)
            off_regs = [pe.alloc_register(f"off{j}") for j in range(J)]

            def attr_T(g, k):
                if not isinstance(g, int) or g <= FULL_G:
                    pe.wait_ge(S_attr[k], landed(g, k) + (16 if isinstance(g, int) and g == FULL_G else 0))
                wait(pe, S["attrT_ready"], g)
                for q in range(2):
                    last = nc.tensor.transpose(pTP[:, q, :], attr[:, k, q * 2 * R:(q + 1) * 2 * R], ident[:, :])
                last.then_inc(S["tp_done"], 1)

            def hidden(g, k):
                pe.wait_ge(S["attrT_ready"], g + 1)
                wait(pe, S["relu_done"], g)
                for h in range(2):
                    last = nc.tensor.matmul(pHID[:, h, :].rearrange("p (q e) -> p q e", q=2), W1s[h * R:(h + 1) * R, :],
                                            attrT[h * R:(h + 1) * R, k % 2, :, :], start=True, stop=True)
                last.then_inc(S["hid_done"], 1)

            def weights(g, k):
                pe.wait_ge(S["relu_done"], g + 1)
                wait(pe, S["msg_done"], g - 1)
                for p_ in range(3):
                    nc.tensor.matmul(pW[:, k % 2, :].rearrange("p (j c) -> p j c", j=J), onesb[0:1, :],
                                     b2p[0:1, p_, :].unsqueeze(1).to_broadcast([1, J, C]), start=(p_ == 0), stop=False)
                for j in range(J):
                    last = nc.tensor.matmul(pW[:, k % 2, j * C:(j + 1) * C], hidT[:, k % 2, j % 2, j // 2, :], W2s[:, :],
                                            start=False, stop=(j == J - 1))
                last.then_inc(S["w_done"], 1)

            def node_rows(g, k):
                pe.load(off_regs, off_i[0:1, ds(g * J, J)])
                pe.wait_ge(S["oht_ready"], g + 1)
                wait(pe, S["hgc_done"], g)
                for j in range(J):
                    at = pe.snap(off_regs[j], min_val=0, max_val=(NB - 1) * 3 * C)
                    for n in range(6):
                        w, a = divmod(n, 3)
                        last = nc.tensor.matmul(pHG[:, j * C:(j + 1) * C], oht[:, k % 2, w, j * P:(j + 1) * P],
                                                h1p[:, ds(at + n * C, C)], start=(n == 0), stop=(n == 5))
                last.then_inc(S["hg_done"], 1)

            def equal_sums(g, k):
                pe.wait_ge(S["msg_done"], g + 1)
                pe.wait_ge(S["eqm_ready"], g + 1)
                wait(pe, S["out_ready"], g - 1)
                for j in range(J):
                    last = nc.tensor.matmul(pDD[:, k % 2, j * C:(j + 1) * C], eqm[:, k % 2, j, :], msg[:, k % 2, j * C:(j + 1) * C],
                                            start=True, stop=True)
                last.then_inc(S["dd_done"], 1)

            attr_T(0, 0)
            attr_T(1, 1)
            hidden(0, 0)

            def layer1(s, k):
                known = isinstance(s, int)
                node_rows(s, k)
                weights(s, k)
                if not known or s + 1 < G:
                    hidden(s + 1, (k + 1) % U)
                if not known or s + 2 < G:
                    attr_T(s + 2, (k + 2) % U)
                if not known or s > 0:
                    equal_sums(s - 1, (k - 1) % U)

            steps(pe, layer1)
            equal_sums(G - 1, (G - 1) % U)

        @block.scalar
        def _(act):
            def squares(c, n):
                act.wait_ge(S["lnT"], n + 1)
                wait(act, S["lnT_copied"], n - 1)
                nc.scalar.activation(E1[:, n % 2, :], H[:, chunk(c), :].rearrange("p b c -> p (b c)"), ACT.Square).then_inc(S["sq_done"], 1)

            def deviations(c, n):
                act.wait_ge(S["lnT_copied"], n + 1)
                nc.scalar.activation(var[:, chunk(c)], var[:, chunk(c)], ACT.Sqrt, bias=epsc[:, :]).then_inc(S["std_ready"], 1)

            for c in range(NCH + 1):
                if c < NCH:
                    squares(c, c)
                if c:
                    deviations(c - 1, c - 1)

            def copy_T(n):
                act.wait_ge(S["hT_done"], n + 1)
                if n >= 2:
                    act.wait_ge(S["z_done" if n - 2 < NCH else "hiT"], n - 1 if n - 2 < NCH else n - 1 - NCH)
                nc.scalar.activation(h0T[:, n % 2, :], psT[:, n % 2, 0:CW], ACT.Copy).then_inc(S["hT_copied"], 1)

            copy_T(0)
            for c in range(NCH):
                if c + 1 < NCH:
                    copy_T(c + 1)
                act.wait_ge(S["zs_ready"], c + 1)
                wait(act, S["sum_ready"], c - 1)
                nc.scalar.activation(E1[:, c % 2, :], H[:, chunk(c), :].rearrange("p b c -> p (b c)"), ACT.Exp).then_inc(S["exp_done"], 1)
                act.wait_ge(S["sum_ready"], c + 1)
                nc.scalar.activation(zsum[:, chunk(c)], zsum[:, chunk(c)], ACT.Ln).then_inc(S["ln_done"], 1)
            for c in range(NCH + 1):
                if c < NCH:
                    squares(c, NCH + c)
                if c:
                    deviations(c - 1, NCH + c - 1)
            for c in range(NCH):
                copy_T(NCH + c)

            act.wait_ge(S["h1_ready"], 1)

            def attrT_copy(g, k):
                act.wait_ge(S["tp_done"], g + 1)
                wait(act, S["hid_done"], g - 1)
                nc.scalar.activation(attrT[:, k % 2, :, :], pTP, ACT.Copy).then_inc(S["attrT_ready"], 1)

            def relu(g, k):
                act.wait_ge(S["hid_done"], g + 1)
                wait(act, S["w_done"], g - 1)
                nc.scalar.activation(hidT[:, k % 2, :, :, :].rearrange("p h q e -> p h (q e)"), pHID, ACT.Relu,
                                     bias=b1c[:, :]).then_inc(S["relu_done"], 1)

            def rows_copy(g, k):
                act.wait_ge(S["hg_done"], g + 1)
                wait(act, S["msg_done"], g - 1)
                nc.scalar.activation(hgs[:, k % 2, :], pHG, ACT.Copy).then_inc(S["hgc_done"], 1)

            attrT_copy(0, 0)
            attrT_copy(1, 1)
            relu(0, 0)

            def layer1(s, k):
                known = isinstance(s, int)
                rows_copy(s, k)
                if not known or s + 1 < G:
                    relu(s + 1, (k + 1) % U)
                if not known or s + 2 < G:
                    attrT_copy(s + 2, (k + 2) % U)

            steps(act, layer1)


_INS = ["x", "src", "dst", "edge_attr_64", "L0_gnn_W_l", "L0_gnn_W_r", "L0_gnn_b", "L1_gnn_W1", "L1_gnn_b1",
        "L1_gnn_W2", "L1_gnn_b2", "L1_gnn_Wl", "L1_gnn_bl"]
_OUTS = [((6250, 128), "float32")]


def kernel(**inputs):
    import numpy as _np
    import concourse.bacc as _bacc
    from concourse import mybir as _mybir
    from concourse.bass_utils import run_bass_kernel_spmd as _run

    nc = _bacc.Bacc("TRN2", target_bir_lowering=False, num_devices=1)
    arrays, args = {}, []
    for name in _INS:
        a = _np.ascontiguousarray(inputs[name])
        arrays[f"in_{name}_dram"] = a
        args.append(nc.dram_tensor(f"in_{name}_dram", a.shape, _mybir.dt.from_np(a.dtype), kind="ExternalInput").ap())
    for i, (shape, dtype) in enumerate(_OUTS):
        dt = _mybir.dt.from_np(_np.dtype(dtype))
        args.append(nc.dram_tensor(f"out_{i}_dram", shape, dt, kind="ExternalOutput").ap())
    gnn_program(nc, *args)
    r = _run(nc, [arrays], core_ids=[0])
    got = tuple(r.results[0][f"out_{i}_dram"] for i in range(len(_OUTS)))
    return got[0]
```

```python
import concourse.bass as bass
from concourse import mybir
from contextlib import ExitStack


def gnn_program(nc, x, src, dst, edge_attr, W_l, W_r, b_0, W1, b1, W2, b2, Wl, bl, out):
    fp32, bf16 = mybir.dt.float32, mybir.dt.bfloat16
    i32, i16 = mybir.dt.int32, mybir.dt.int16
    ALU = mybir.AluOpType
    ACT = mybir.ActivationFunctionType
    AX = mybir.AxisListType.X
    ds = bass.ds

    P = 128
    N, C = x.shape
    E, R = edge_attr.shape
    EPS = 1e-5
    NB = -(-N // P)
    NP = NB * P
    CB = 7
    NCH = NB // CB
    assert NCH * CB == NB and CB <= 8
    CW = CB * P
    NTAIL = N - (NB - 1) * P
    J = 4
    GE = J * P
    U = 4
    G = -(-E // GE)
    G += -G % U
    T = G * J
    TB = -(-T // P)
    TP = TB * P
    FULL_G = E // GE
    LAST_T = E - FULL_G * GE
    FULL_TB = E // (P * P)
    LAST_ROWS = (E - FULL_TB * P * P) // P
    LAST_COLS = E % P
    AGW = NP + P
    DUMP = NP
    ACCR = NP + P
    NACC = 2 * J
    NO_NODE = 30000

    h0_d = nc.dram_tensor("h0_rows", (NP, C), fp32).ap()
    rows_d = nc.dram_tensor("edge_rows", (2, TP * P), i16).ap()
    acc_d = [nc.dram_tensor(f"acc{i}", (ACCR, C), fp32).ap() for i in range(NACC)]

    ctx = ExitStack()
    with ctx:
        def sb(name, shape, dt):
            return ctx.enter_context(nc.sbuf_tensor(name, shape, dt))

        def pb(name, shape, dt):
            return ctx.enter_context(nc.psum_tensor(name, shape, dt))

        def sem(name):
            return ctx.enter_context(nc.semaphore(name))

        X = sb("X", [P, NB, C], fp32)
        H = sb("H", [P, NB, C], fp32)
        E1 = sb("E1", [P, 2, CW], fp32)
        srccol = sb("srccol", [P, TP], fp32)
        dstloc = sb("dstloc", [P, TP], fp32)
        idx = sb("idx", [P, TP], i32)
        dup = sb("dup", [P, TP], fp32)
        rows = sb("rows", [P, U, 2, GE], i16)
        idxr = sb("idxr", [P, U, J], i32)
        ident = sb("ident", [P, P], fp32)
        iotaF = sb("iotaF", [P, P], fp32)
        iotaP = sb("iotaP", [P, 4], fp32)
        tri = sb("tri", [P, P], bf16)
        onesf = sb("onesf", [P, P], fp32)
        onesb = sb("onesb", [P, P], bf16)
        Wraw = sb("Wraw", [P, 2, C], fp32)
        WlrT = sb("WlrT", [P, 2, C], fp32)
        Wh = sb("Wh", [P, C], fp32)
        W1s = sb("W1s", [P, C], fp32)
        W2s = sb("W2s", [P, C], fp32)
        b1c = sb("b1c", [P, 1], fp32)
        brow = sb("brow", [1, 2, C], fp32)
        h0T = sb("h0T", [P, 2, CW], fp32)
        mean = sb("mean", [P, NB], fp32)
        var = sb("var", [P, NB], fp32)
        zmax = sb("zmax", [P, NB], fp32)
        zsum = sb("zsum", [P, NB], fp32)
        epsc = sb("epsc", [P, 1], fp32)

        big = sb("big", [P, 2 * AGW], fp32)
        agg = big[:, :].rearrange("p (a n) -> p a n", a=2)
        used = [0]

        def part(base, cursor, width):
            at = cursor[0]
            cursor[0] += width
            assert cursor[0] <= base.shape[1], (cursor, base.shape)
            return base[:, at:at + width]

        attr = part(big, used, U * J * R).rearrange("p (u f) -> p u f", u=U)
        attrT = part(big, used, 2 * 2 * P).rearrange("p (s q e) -> p s q e", s=2, q=2)
        hidT = part(big, used, 2 * GE).rearrange("p (s h q e) -> p s h q e", s=2, h=2, q=2)
        eqm = part(big, used, 2 * GE).rearrange("p (s j e) -> p s j e", s=2, j=J)
        hgs = part(big, used, 2 * GE).rearrange("p (s f) -> p s f", s=2)
        msg = part(big, used, 2 * GE).rearrange("p (s f) -> p s f", s=2)
        outr = part(big, used, U * GE).rearrange("p (u j c) -> p u j c", u=U, j=J)
        oht = part(big, used, 2 * GE).bitcast(bf16).rearrange("p (s w f) -> p s w f", s=2, w=2)

        par = sb("par", [P, (NB + 1) * 3 * C], bf16)
        h1p = par[:, :]
        parf = par[:, :].bitcast(fp32)
        ubs = [0]
        raw = part(parf, ubs, 2 * TP).bitcast(i32).rearrange("p (w b e) -> p w b e", w=2, b=TB)
        r16 = part(parf, ubs, TP).bitcast(i16).rearrange("p (w b e) -> p w b e", w=2, b=TB)
        Grow = part(parf, ubs, U * J * C).rearrange("p (u j c) -> p u j c", u=U, j=J)
        oh = part(parf, ubs, 2 * GE).rearrange("p (s j n) -> p s j n", s=2, j=J)
        rawf = H[:, :, :].rearrange("p b c -> p (b c)")[:, 0:2 * TP].rearrange("p (w b e) -> p w b e", w=2, b=TB)
        eqb = sb("eqb", [P, 2, 2, J, P], bf16)
        base_i = E1[:, :, :].rearrange("p a b -> p (a b)")[0:1, 0:TP].bitcast(i32)
        base_b = sb("base_b", [P, TB], i32)
        base_f = sb("base_f", [P, TB], fp32)
        off_i = dstloc[:, :].bitcast(i32)
        b2x = sb("b2x", [3, C], fp32)
        b2s = sb("b2s", [3, 3, C], bf16)
        b2p = sb("b2p", [3, C], bf16)
        zeros = sb("zeros", [P, 5 * C], fp32)

        PS = pb("PS", [P, 8, 512], fp32)

        psA = PS[:, 0:4, :].rearrange("p b f -> p (b f)").rearrange("p (s a j n) -> p s a j n", s=2, a=2, j=J)
        psD = PS[:, 4:6, 0:J]
        psZ = PS[:, 0:4, :].rearrange("p (s b) f -> p s (b f)", s=2)
        psZ0, psZ1 = psZ[:, 0, :], psZ[:, 1, :]
        psT = PS[:, 4:8, :].rearrange("p (s b) f -> p s (b f)", s=2)
        pTP = PS[:, 0, 0:2 * P].rearrange("p (q e) -> p q e", q=2)
        pHID = PS[:, 1:3, 0:2 * P]
        pW = PS[:, 3:5, :]
        pHG = PS[:, 5, :]
        pDD = PS[:, 6:8, :]

        names = """x_in raw_in w_in consts cast_done colT_done big_zero srccol_ready dstcol_ready bcast_done tables_ready
            rows16_ready rows_out zero_ready acc0_x h0_ready h0_out sq_done sq1 std_ready std1 wT_done wT_ready
            idx_ready sums_done oh_ready eq_ready dups_done dup_copied agg_done eqtri_done
            aggn_ready h0T_done h0T_copied h1T_done h1T_copied z_done zs_ready exp_done sum_ready ln_done x1_ready
            h1a_ready prod_done part0_ready part1_ready rest_ready parts_ready rings_free off_ready tail_in d_consts b2_ready
            tp_done attrT_ready hid_done relu_done w_done hg_done hgc_done oht_ready eqm_ready msg_done dd_done
            out_ready fin_in0 fin_in1 fin_done out_done0 out_done1 chain pool_c lnT lnT_copied hw_done hw_copied adj_ready""".split()
        S = {n: sem(n) for n in names}
        S_gat = [[sem(f"gathered_{k}_{j}") for j in range(J)] for k in range(U)]
        S_srow = [sem(f"src_row_in_{k}") for k in range(U)]
        S_rows = [sem(f"rows_in_{k}") for k in range(U)]
        S_attr = [sem(f"attr_in_{k}") for k in range(U)]
        S_acc = [sem(f"acc_added_{h}") for h in range(2)]
        S_zero = sem("acc_zeroed")

        def wait(eng, s, v):
            if not (isinstance(v, int) and v <= 0):
                eng.wait_ge(s, v)

        def landed(s, k):
            return 4 * (s - k) + 16

        assert U == 4

        def steps(eng, step, rings=3):
            assert (G // U - 2) % rings == 0
            for s in range(U):
                step(s, s)
            with eng.Fori(0, (G // U - 2) // rings) as i:
                for k in range(U * rings):
                    step(i * (U * rings) + (U + k), k % U)
            for s in range(G - U, G):
                step(s, s % U)

        def chunk(c):
            return slice(c * CB, (c + 1) * CB)

        FP = 125
        FN, FB = N // FP, 5
        FW = FB * C
        fin = big[0:FP, 0:2 * NACC * FW].rearrange("p (s a f) -> p s a f", s=2, a=NACC)
        fino = X[:, :, :].rearrange("p b c -> p (b c)")[0:FP, 0:2 * FW].rearrange("p (s f) -> p s f", s=2)
        less_dump = E1[:, :, :].rearrange("p a b -> p (a b)")
        assert TP <= 2 * CW
        NTR = -(-TB // 4)
        ZPARTS = ACCR // P // 5
        assert 5 * (NACC - 1) * ZPARTS < G

        block = ctx.enter_context(nc.Block())

        @block.sync
        def _(sp):
            sp.wait_ge(S["zero_ready"], 1)
            for c in range(NCH):
                lo, hi = c * CB, min((c + 1) * CB, NB - 1)
                sp.dma_start(X[:, lo:hi, :], x[lo * P:hi * P, :].rearrange("(b p) c -> p b c", p=P)).then_inc(S["x_in"], 16)
                if c == NCH - 1:
                    sp.dma_start(X[0:NTAIL, NB - 1, :], x[(NB - 1) * P:N, :]).then_inc(S["tail_in"], 16)
                sp.wait_ge(S["x_in"], 16 * (c + 1))
            sp.dma_start(W1s[0:R, :], W1).then_inc(S["w_in"], 16)
            sp.dma_start(W1s[R:2 * R, :], W1).then_inc(S["w_in"], 16)
            sp.dma_start(W2s[:, :], W2).then_inc(S["w_in"], 16)
            sp.dma_start(Wraw[:, 0, :], W_l).then_inc(S["w_in"], 16)
            sp.dma_start(Wraw[:, 1, :], W_r).then_inc(S["w_in"], 16)
            sp.dma_start(Wh[:, :], Wl).then_inc(S["w_in"], 16)
            sp.dma_start(b1c[:, :], b1.rearrange("(p a) -> p a", a=1)).then_inc(S["w_in"], 16)
            for n, v in enumerate((b_0, bl)):
                sp.dma_start(brow[:, n, :], v.rearrange("(a c) -> a c", a=1)).then_inc(S["w_in"], 16)
            sp.dma_start(b2x[:, :], b2.partition_broadcast(3)).then_inc(S["w_in"], 16)
            for c in range(NCH):
                sp.wait_ge(S["h0_ready"], c + 1)
                sp.dma_start(h0_d[c * CW:(c + 1) * CW, :].rearrange("(b p) c -> p b c", p=P),
                             H[:, chunk(c), :]).then_inc(S["h0_out"], 16)
            sp.wait_ge(S["rows16_ready"], 1)
            for w in range(2):
                sp.dma_start(rows_d[w, :].rearrange("(b p e) -> p b e", p=P, e=P), r16[:, w, :, :]).then_inc(S["rows_out"], 16)
            sp.wait_ge(S["rows_out"], 32)

            def src_row(g, k):
                wait(sp, S["eq_ready"], g - U + 1)
                sp.dma_start(rows[:, k, 1, :], rows_d[1, ds(g * GE, GE)].partition_broadcast(P)).then_inc(S_srow[k], 16)

            steps(sp, src_row)

            for c in range(NCH):
                sp.wait_ge(S["x1_ready"], c + 1)
                hi = min((c + 1) * CB, NB - 1)
                sp.dma_start(acc_d[0][c * CW:hi * P, :].rearrange("(b p) c -> p b c", p=P),
                             X[:, c * CB:hi, :]).then_inc(S["acc0_x"], 16)
            sp.dma_start(acc_d[0][hi * P:N, :], X[0:NTAIL, NB - 1, :]).then_inc(S["acc0_x"], 16)

            def edge_loads(g, k):
                wait(sp, S["eqm_ready"], g - U + 1)
                wait(sp, S["oht_ready"], g - U + 1)
                sp.dma_start(rows[:, k, :, :], rows_d[:, ds(g * GE, GE)].partition_broadcast(P)).then_inc(S_rows[k], 16)
                wait(sp, S["tp_done"], g - U + 1)
                if not isinstance(g, int) or g < FULL_G:
                    sp.dma_start(attr[:, k, :].rearrange("p (j f) -> p j f", j=J),
                                 edge_attr[ds(g * GE, GE), :].rearrange("(j p) f -> p j f", p=P)).then_inc(S_attr[k], 16)
                elif g == FULL_G:
                    full = LAST_T // P
                    sp.dma_start(attr[:, k, 0:full * R].rearrange("p (j f) -> p j f", j=full),
                                 edge_attr[g * GE:g * GE + full * P, :].rearrange("(j p) f -> p j f", p=P)).then_inc(S_attr[k], 16)
                    sp.dma_start(attr[0:LAST_T - full * P, k, full * R:(full + 1) * R],
                                 edge_attr[g * GE + full * P:E, :]).then_inc(S_attr[k], 16)

            sp.wait_ge(S["rings_free"], 1)
            steps(sp, edge_loads)
            for h in range(2):
                sp.wait_ge(S_acc[h], 16 * J * G // 2)
            for c in range(FN // FB):
                if c >= 2:
                    sp.wait_ge(S["fin_done"], c - 1)
                for a in range(NACC):
                    sp.dma_start(fin[:, c % 2, a, :], acc_d[a][0:N, :].rearrange("(p b) c -> p (b c)", p=FP)
                                 [:, c * FB * C:(c + 1) * FB * C]).then_inc(S[f"fin_in{c % 2}"], 16)
                if c >= 1:
                    sp.wait_ge(S["fin_done"], c)
                    sp.dma_start(out.rearrange("(p b) c -> p (b c)", p=FP)[:, (c - 1) * FB * C:c * FB * C],
                                 fino[:, (c - 1) % 2, :]).then_inc(S[f"out_done{(c - 1) % 2}"], 16)
            last = FN // FB - 1
            sp.wait_ge(S["fin_done"], last + 1)
            sp.dma_start(out.rearrange("(p b) c -> p (b c)", p=FP)[:, last * FB * C:(last + 1) * FB * C],
                         fino[:, last % 2, :]).then_inc(S[f"out_done{last % 2}"], 16)
            for c in range(2):
                sp.wait_ge(S[f"out_done{c}"], 16 * ((last + 2 - c) // 2))

        @block.gpsimd
        def _(pool):
            pool.memset(X[:, NB - 1, :], 0.0).then_inc(S["zero_ready"], 1)
            pool.memset(raw[:, 0, TB - 1, :], NO_NODE).then_inc(S["pool_c"], 1)
            pool.memset(raw[:, 1, TB - 1, :], N).then_inc(S["pool_c"], 1)
            pool.wait_ge(S["pool_c"], 2)
            for w, v in enumerate((dst, src)):
                pool.dma_start(raw[:, w, 0:FULL_TB, :], v[0:FULL_TB * P * P].rearrange("(b p e) -> p b e", p=P, e=P)).then_inc(S["raw_in"], 16)
                at = FULL_TB * P * P
                pool.dma_start(raw[0:LAST_ROWS, w, FULL_TB, :], v[at:at + LAST_ROWS * P].rearrange("(p e) -> p e", e=P)).then_inc(S["raw_in"], 16)
                at += LAST_ROWS * P
                pool.dma_start(raw[LAST_ROWS:LAST_ROWS + 1, w, FULL_TB, 0:LAST_COLS],
                               v[at:E].rearrange("(a e) -> a e", a=1)).then_inc(S["raw_in"], 16)
            pool.iota(iotaF[:, :], pattern=[[1, P]], base=0, channel_multiplier=0, allow_small_or_imprecise_dtypes=True).then_inc(S["consts"], 1)
            pool.iota(iotaP[:, 0:2], pattern=[[P, 2]], base=0, channel_multiplier=1, allow_small_or_imprecise_dtypes=True).then_inc(S["consts"], 1)
            pool.iota(iotaP[:, 2:3], pattern=[[1, 1]], base=DUMP, channel_multiplier=1, allow_small_or_imprecise_dtypes=True).then_inc(S["consts"], 1)
            pool.memset(onesf[:, :], 1.0).then_inc(S["consts"], 1)
            pool.memset(onesb[:, :], 1.0).then_inc(S["consts"], 1)
            pool.memset(epsc[:, :], EPS).then_inc(S["consts"], 1)
            pool.memset(zeros[:, :], 0.0).then_inc(S["consts"], 1)
            pool.memset(big[:, :], 0.0).then_inc(S["big_zero"], 1)
            filled = pool.alloc_register("filled")

            def turns(semaphore, per_wait, body, start):
                def some(g, k, straight):
                    if straight:
                        pool.wait_ge(semaphore, g + per_wait)
                    else:
                        pool.wait_ge(semaphore, filled)
                        pool.reg_add(filled, filled, per_wait)
                    for n in range(per_wait):
                        start((k + n) % U)

                for g in range(0, U, per_wait):
                    some(g, g % U, True)
                pool.reg_mov(filled, U + per_wait)
                with pool.Fori(0, (G - U) // body):
                    for k in range(0, body, per_wait):
                        some(None, k % U, False)
                for g in range(G - (G - U) % body, G, per_wait):
                    some(g, g % U, True)

            pool.wait_ge(S["h0_out"], 16 * NCH)

            def gather(k):
                for j in range(J):
                    pool.indirect_dma_start(Grow[:, k, j, :], None, h0_d,
                                            bass.IndirectOffsetOnAxis(ap=idxr[:, k, j:j + 1], axis=0)).then_inc(S_gat[k][j], 16)

            turns(S["idx_ready"], 2, 4 * U, gather)
            for c in range(NCH):
                pool.wait_ge(S["ln_done"], c + 1)
                nc.gpsimd.tensor_tensor(H[:, chunk(c), :], H[:, chunk(c), :],
                                        zsum[:, chunk(c)].unsqueeze(2).to_broadcast([P, CB, P]), ALU.subtract).then_inc(S["pool_c"], 1)
                pool.wait_ge(S["pool_c"], 2 + c + 1)
                nc.gpsimd.tensor_tensor(X[:, chunk(c), :], X[:, chunk(c), :], H[:, chunk(c), :], ALU.add).then_inc(S["x1_ready"], 1)
            pool.wait_ge(S_zero, 16 * ((NACC - 1) * ZPARTS + 2))
            pool.wait_ge(S["acc0_x"], 16 * (NCH + 1))

            def scatter(k):
                for j in range(J):
                    pool.indirect_dma_start(acc_d[J * (k % 2) + j], bass.IndirectOffsetOnAxis(ap=idxr[:, k, j:j + 1], axis=0),
                                            outr[:, k, j, :], None, compute_op=ALU.add).then_inc(S_acc[k % 2], 16)

            turns(S["out_ready"], 1, 4 * U, scatter)

        def dve_link(eng):
            count = [0]

            def link(ins):
                count[0] += 1
                ins.then_inc(S["chain"], 1)
                eng.wait_ge(S["chain"], count[0])
            return link

        @block.vector
        def _(dve):
            link = dve_link(dve)

            def bc(col):
                return col.unsqueeze(2).to_broadcast([P, CB, P])

            dve.wait_ge(S["consts"], 7)
            nc.vector.tensor_scalar(ident[:, :], iotaF[:, :], iotaP[:, 0:1], None, ALU.is_equal).then_inc(S["d_consts"], 1)
            nc.vector.tensor_scalar(tri[:, :], iotaF[:, :], iotaP[:, 0:1], None, ALU.is_gt).then_inc(S["d_consts"], 1)

            dve.wait_ge(S["raw_in"], 96)
            nc.vector.tensor_copy(rawf[:, 0, :, :], raw[:, 0, :, :]).then_inc(S["cast_done"], 1)
            nc.vector.tensor_copy(rawf[:, 1, :, :], raw[:, 1, :, :]).then_inc(S["cast_done"], 1)
            nc.vector.tensor_copy(r16[:, 1, :, :], raw[:, 1, :, :])
            link(nc.vector.tensor_scalar(base_b[:, :], raw[:, 0, :, 0], -P, None, ALU.bitwise_and))
            link(nc.vector.tensor_copy(base_f[:, :], base_b[:, :]))
            dve.wait_ge(S["cast_done"], 2)
            nc.vector.tensor_tensor(r16[:, 0, :, :], rawf[:, 0, :, :], base_f[:, :].unsqueeze(2).to_broadcast([P, TB, P]),
                                    ALU.subtract).then_inc(S["rows16_ready"], 1)
            for n in range(2 * NTR):
                w, q = divmod(n, NTR)
                blocks = min(4, TB - 4 * q)
                dve.wait_ge(S["colT_done"], n + 1)
                ps = psT[:, n % 2, 0:blocks * P]
                to = (dstloc, srccol)[w][:, 4 * q * P:4 * q * P + blocks * P]
                nc.vector.tensor_copy(to, ps).then_inc(S["dstcol_ready" if w == 0 else "srccol_ready"], 1)
            dve.wait_ge(S["srccol_ready"], NTR)
            nc.vector.tensor_copy(idx[:, :], srccol[:, :]).then_inc(S["tables_ready"], 1)

            def norm_mean(c):
                link(nc.vector.tensor_reduce(mean[:, chunk(c)], X[:, chunk(c), :], AX, ALU.add))
                link(nc.vector.tensor_scalar(mean[:, chunk(c)], mean[:, chunk(c)], 1.0 / C, None, ALU.mult))
                nc.vector.tensor_tensor(H[:, chunk(c), :], X[:, chunk(c), :], bc(mean[:, chunk(c)]), ALU.subtract)\
                    .then_inc(S["lnT"], 1)

            def norm_var(c, n, slot):
                dve.wait_ge(S["sq_done"], n + 1)
                link(nc.vector.tensor_reduce(var[:, chunk(c)], E1[:, slot, :].rearrange("p (b c) -> p b c", c=C), AX, ALU.add))
                nc.vector.tensor_scalar(var[:, chunk(c)], var[:, chunk(c)], 1.0 / C, None, ALU.mult).then_inc(S["lnT_copied"], 1)

            def norm_relu(c, n, ready):
                dve.wait_ge(S["std_ready"], n + 1)
                link(nc.vector.reciprocal(var[:, chunk(c)], var[:, chunk(c)]))
                nc.vector.scalar_tensor_tensor(out=H[:, chunk(c), :], in0=H[:, chunk(c), :], scalar=0.0,
                                               in1=bc(var[:, chunk(c)]), op0=ALU.max, op1=ALU.mult).then_inc(S[ready], 1)

            dve.wait_ge(S["colT_done"], 2 * NTR)
            for c in range(NCH + 2):
                if c < NCH:
                    dve.wait_ge(S["x_in"], 16 * (c + 1))
                    if c == NCH - 1:
                        dve.wait_ge(S["tail_in"], 16)
                    norm_mean(c)
                if c > 1:
                    norm_relu(c - 2, c - 2, "h0_ready")
                if 0 < c <= NCH:
                    norm_var(c - 1, c - 1, (c - 1) % 2)

            link(nc.vector.tensor_copy(base_i, dstloc[0:1, :]))
            link(nc.vector.memset(base_i[:, T - (T - -(-E // P)):TP], 0))
            for q in range(NTR):
                w = min(512, TP - q * 512)
                dve.wait_ge(S["bcast_done"], q + 1)
                link(nc.vector.tensor_tensor(dstloc[:, q * 512:q * 512 + w], dstloc[:, q * 512:q * 512 + w],
                                             psZ[:, q // 2, (q % 2) * 512:(q % 2) * 512 + w], ALU.subtract))
            link(nc.vector.memset(dstloc[:, -(-E // P):TP], float(NO_NODE)))

            dve.wait_ge(S["wT_done"], 1)
            nc.vector.tensor_copy(WlrT[:, :, :], psT[:, 0, 0:2 * C].rearrange("p (w c) -> p w c", w=2)).then_inc(S["wT_ready"], 1)
            dve.wait_ge(S["w_in"], 160)
            for q in range(3):
                link(nc.vector.tensor_copy(b2s[:, q, :], b2x[:, :]))
                link(nc.vector.tensor_tensor(b2x[:, :], b2x[:, :], b2s[:, q, :], ALU.subtract))
            link(nc.vector.tensor_scalar(b2p[:, :], b2s[:, 0, :], ident[0:3, 0:1], None, ALU.mult))
            for q in range(1, 3):
                link(nc.vector.scalar_tensor_tensor(out=b2p[:, :], in0=b2s[:, q, :], scalar=ident[0:3, q:q + 1], in1=b2p[:, :],
                                                    op0=ALU.mult, op1=ALU.add))

            def idx_columns(g, k):
                nc.vector.tensor_copy(idxr[:, k, :], idx[:, ds(g * J, J)]).then_inc(S["idx_ready"], 1)

            def one_hot(g, k):
                wait(dve, S["sums_done"], g - 1)
                nc.vector.tensor_tensor(oh[:, k % 2, :, :], iotaF[:, :].unsqueeze(1).to_broadcast([P, J, P]),
                                        dstloc[:, ds(g * J, J)].unsqueeze(2).to_broadcast([P, J, P]), ALU.is_equal)\
                    .then_inc(S["oh_ready"], 1)

            def equals(g, k):
                dve.wait_ge(S_srow[k], landed(g, k))
                nc.vector.tensor_tensor(eqb[:, k % 2, 0, :, :], rows[:, k, 1, :].rearrange("p (j e) -> p j e", j=J),
                                        srccol[:, ds(g * J, J)].unsqueeze(2).to_broadcast([P, J, P]), ALU.is_equal)\
                    .then_inc(S["eq_ready"], 1)

            def equals_before(g, k):
                dve.wait_ge(S["eq_ready"], g + 1)
                wait(dve, S["dups_done"], g - 1)
                nc.vector.tensor_tensor(eqb[:, k % 2, 1, :, :], eqb[:, k % 2, 0, :, :],
                                        tri[:, :].unsqueeze(1).to_broadcast([P, J, P]), ALU.mult).then_inc(S["eqtri_done"], 1)

            base_regs = [dve.alloc_register(f"base{j}") for j in range(J)]

            def first_nodes(g):
                dve.load(base_regs, base_i[0:1, ds(g * J, J)])
                return [dve.snap(r, min_val=0, max_val=NP) for r in base_regs]

            def add_sum(g, k, j, at):
                wait(dve, S["agg_done"], g * J + j)
                nc.vector.tensor_tensor(agg[:, :, ds(at, P)], agg[:, :, ds(at, P)], psA[:, k % 2, :, j, :], ALU.add)\
                    .then_inc(S["agg_done"], 1)

            def dup_counts(g, k):
                dve.wait_ge(S["dups_done"], g + 1)
                nc.vector.tensor_copy(dup[:, ds(g * J, J)], psD[:, k % 2, :]).then_inc(S["dup_copied"], 1)

            for g in range(U):
                idx_columns(g, g)
            one_hot(0, 0)
            dve.wait_ge(S["big_zero"], 1)
            equals(0, 0)
            equals_before(0, 0)

            def layer0(s, k):
                known = isinstance(s, int)
                first = first_nodes(s)
                dve.wait_ge(S["sums_done"], s + 1)
                if not known or s + U < G:
                    idx_columns(s + U, k)
                for j, at in enumerate(first):
                    add_sum(s, k, j, at)
                    if j < J - 1 and (not known or s + 1 < G):
                        (one_hot, equals, equals_before)[j](s + 1, (k + 1) % U)
                dup_counts(s, k)

            steps(dve, layer0)

            dve.wait_ge(S["agg_done"], T)
            dve.wait_ge(S["dup_copied"], G)
            link(nc.vector.tensor_scalar(off_i[0:1, 0:TP], base_i, -P, None, ALU.bitwise_and))
            link(nc.vector.tensor_scalar(off_i[0:1, 0:TP], off_i[0:1, 0:TP], float(3 * C // P), None, ALU.mult))
            link(nc.vector.tensor_scalar(dup[:, 0:T], dup[:, 0:T], 1.0, None, ALU.min))
            link(nc.vector.scalar_tensor_tensor(out=less_dump[:, 0:T], in0=srccol[:, 0:T], scalar=iotaP[:, 2:3], in1=dup[:, 0:T],
                                                op0=ALU.subtract, op1=ALU.mult))
            link(nc.vector.tensor_tensor(idx[:, 0:T], srccol[:, 0:T], less_dump[:, 0:T], ALU.subtract))
            for g in range(U):
                nc.vector.tensor_copy(idxr[:, g, :], idx[:, g * J:(g + 1) * J]).then_inc(S["adj_ready"], 1)

            def means(c):
                w = slice(c * CW, (c + 1) * CW)
                link(nc.vector.tensor_scalar(agg[:, 1, w], agg[:, 1, w], 1.0, None, ALU.max))
                link(nc.vector.reciprocal(agg[:, 1, w], agg[:, 1, w]))
                nc.vector.tensor_tensor(agg[:, 0, w], agg[:, 0, w], agg[:, 1, w], ALU.mult).then_inc(S["aggn_ready"], 1)

            def blocks(ps):
                return ps[:, 0:CW].rearrange("p (b c) -> p b c", c=C)

            def logits(c):
                dve.wait_ge(S["z_done"], c + 1)
                link(nc.vector.tensor_reduce(zmax[:, chunk(c)], blocks(psZ0), AX, ALU.max))
                nc.vector.tensor_tensor(H[:, chunk(c), :], blocks(psZ0), bc(zmax[:, chunk(c)]), ALU.subtract).then_inc(S["zs_ready"], 1)

            def softmax_sum(c):
                dve.wait_ge(S["exp_done"], c + 1)
                nc.vector.tensor_reduce(zsum[:, chunk(c)], E1[:, 0, :].rearrange("p (b c) -> p b c", c=C), AX, ALU.add)\
                    .then_inc(S["sum_ready"], 1)

            hp = h1p.rearrange("p (b a c) -> p b a c", a=3, c=C)

            def first_rest(c):
                dve.wait_ge(S["part0_ready"], c + 1)
                nc.vector.tensor_tensor(H[:, chunk(c), :], blocks(psZ1), hp[:, chunk(c), 0, :], ALU.subtract).then_inc(S["rest_ready"], 1)

            def last_part(c):
                dve.wait_ge(S["part1_ready"], c + 1)
                nc.vector.tensor_tensor(hp[:, chunk(c), 2, :], H[:, chunk(c), :], hp[:, chunk(c), 1, :], ALU.subtract)\
                    .then_inc(S["parts_ready"], 1)

            nc.vector.memset(hp[:, NB, :, :], 0.0).then_inc(S["parts_ready"], 1)
            for i in range(NCH + 9):
                if i < NCH:
                    means(i)
                if 0 <= i - 1 < NCH:
                    logits(i - 1)
                if 0 <= i - 2 < NCH:
                    softmax_sum(i - 2)
                if 0 <= i - 3 < NCH:
                    dve.wait_ge(S["x1_ready"], i - 3 + 1)
                    norm_mean(i - 3)
                if 0 <= i - 4 < NCH:
                    norm_var(i - 4, NCH + i - 4, 1)
                if 0 <= i - 5 < NCH:
                    norm_relu(i - 5, NCH + i - 5, "h1a_ready")
                if i == NCH:
                    dve.wait_ge(S["z_done"], NCH)
                    nc.vector.memset(attr, 0.0).then_inc(S["rings_free"], 1)
                if 0 <= i - 7 < NCH:
                    first_rest(i - 7)
                if 0 <= i - 8 < NCH:
                    last_part(i - 8)
            dve.wait_ge(S["parts_ready"], NCH + 1)

            def one_hot_T(g, k):
                dve.wait_ge(S_rows[k], landed(g, k))
                wait(dve, S["hg_done"], g - 1)
                for w in range(2):
                    last = nc.vector.tensor_scalar(oht[:, k % 2, w, :], rows[:, k, 0, :], iotaP[:, w:w + 1], None, ALU.is_equal)
                last.then_inc(S["oht_ready"], 1)

            def equality(g, k):
                wait(dve, S["dd_done"], g - 1)
                nc.vector.tensor_tensor(eqm[:, k % 2, :, :], rows[:, k, 1, :].rearrange("p (j e) -> p j e", j=J),
                                        srccol[:, ds(g * J, J)].unsqueeze(2).to_broadcast([P, J, P]), ALU.is_equal)\
                    .then_inc(S["eqm_ready"], 1)

            def messages(g, k):
                dve.wait_ge(S["w_done"], g + 1)
                dve.wait_ge(S["hgc_done"], g + 1)
                wait(dve, S["dd_done"], g - 1)
                nc.vector.tensor_tensor(msg[:, k % 2, :], pW[:, k % 2, :], hgs[:, k % 2, :], ALU.mult).then_inc(S["msg_done"], 1)

            def sums_out(g, k):
                dve.wait_ge(S["dd_done"], g + 1)
                wait(dve, S_acc[k % 2], 16 * J // 2 * (g - k % 2))
                nc.vector.tensor_copy(idxr[:, k, :], idx[:, ds(g * J, J)])
                nc.vector.tensor_copy(outr[:, k, :, :], pDD[:, k % 2, :].rearrange("p (j c) -> p j c", j=J)).then_inc(S["out_ready"], 1)

            one_hot_T(0, 0)
            equality(0, 0)

            def layer1(s, k):
                if not isinstance(s, int) or s + 1 < G:
                    one_hot_T(s + 1, (k + 1) % U)
                    equality(s + 1, (k + 1) % U)
                messages(s, k)
                if not isinstance(s, int) or s > 0:
                    sums_out(s - 1, (k - 1) % U)

            steps(dve, layer1)
            sums_out(G - 1, (G - 1) % U)

            for c in range(FN // FB):
                dve.wait_ge(S[f"fin_in{c % 2}"], 16 * NACC * (c // 2 + 1))
                for n in (NACC // 2, NACC // 4):
                    link(nc.vector.tensor_tensor(fin[:, c % 2, 0:n, :], fin[:, c % 2, 0:n, :], fin[:, c % 2, n:2 * n, :], ALU.add))
                if c >= 2:
                    dve.wait_ge(S[f"out_done{c % 2}"], 16 * (c // 2))
                nc.vector.tensor_tensor(fino[:, c % 2, :], fin[:, c % 2, 0, :], fin[:, c % 2, 1, :], ALU.add).then_inc(S["fin_done"], 1)

        @block.tensor
        def _(pe):
            pe.wait_ge(S["d_consts"], 2)
            pe.wait_ge(S["cast_done"], 2)
            for n in range(2 * NTR):
                w, q = divmod(n, NTR)
                wait(pe, S["dstcol_ready"], min(n - 1, NTR))
                wait(pe, S["srccol_ready"], n - 1 - NTR)
                for i in range(min(4, TB - 4 * q)):
                    last = nc.tensor.transpose(psT[:, n % 2, i * P:(i + 1) * P], rawf[:, w, 4 * q + i, :], ident[:, :])
                last.then_inc(S["colT_done"], 1)
            pe.wait_ge(S["dstcol_ready"], NTR)
            for q in range(NTR):
                w = min(512, TP - q * 512)
                nc.tensor.matmul(psZ[:, q // 2, (q % 2) * 512:(q % 2) * 512 + w], onesf[0:1, :], dstloc[0:1, q * 512:q * 512 + w],
                                 start=True, stop=True).then_inc(S["bcast_done"], 1)
            pe.wait_ge(S["srccol_ready"], NTR)
            pe.wait_ge(S["w_in"], 160)
            for w in range(2):
                last = nc.tensor.transpose(psT[:, 0, w * C:(w + 1) * C], Wraw[:, w, :], ident[:, :])
            last.then_inc(S["wT_done"], 1)
            pe.wait_ge(S["wT_ready"], 1)

            def layer0(g, k):
                pe.wait_ge(S["oh_ready"], g + 1)
                wait(pe, S["agg_done"], J * (g - 1))
                nc.tensor.matmul(psA[:, k % 2, 1, :, :], onesf[:, :], oh[:, k % 2, :, :], start=True, stop=True)
                for j in range(J):
                    pe.wait_ge(S_gat[k][j], landed(g, k))
                    last = nc.tensor.matmul(psA[:, k % 2, 0, j, :], Grow[:, k, j, :], oh[:, k % 2, j, :], start=True, stop=True)
                last.then_inc(S["sums_done"], 1)
                pe.wait_ge(S["eqtri_done"], g + 1)
                wait(pe, S["dup_copied"], g - 1)
                for j in range(J):
                    last = nc.tensor.matmul(psD[:, k % 2, j:j + 1], eqb[:, k % 2, 1, j, :], onesb[:, 0:1], start=True, stop=True)
                last.then_inc(S["dups_done"], 1)

            steps(pe, layer0)

            def transposes(c, slot, done):
                for i in range(CB):
                    last = nc.tensor.transpose(psT[:, slot, i * P:(i + 1) * P], H[:, c * CB + i, :], ident[:, :])
                last.then_inc(S[done], 1)

            def layer0_products(c):
                pe.wait_ge(S["aggn_ready"], c + 1)
                pe.wait_ge(S["h0T_copied"], c + 1)
                wait(pe, S["zs_ready"], c)
                for i in range(CB):
                    z = psZ0[:, i * P:(i + 1) * P]
                    n0 = (c * CB + i) * P
                    nc.tensor.matmul(z, agg[:, 0, n0:n0 + P], WlrT[:, 0, :], start=True, stop=False)
                    nc.tensor.matmul(z, h0T[:, 0, i * P:(i + 1) * P], WlrT[:, 1, :], start=False, stop=False)
                    last = nc.tensor.matmul(z, onesf[0:1, :], brow[0:1, 0, :], start=False, stop=True)
                last.then_inc(S["z_done"], 1)

            def layer1_product(c):
                pe.wait_ge(S["h1T_copied"], c + 1)
                wait(pe, S["rest_ready"], c)
                for i in range(CB):
                    z = psZ1[:, i * P:(i + 1) * P]
                    nc.tensor.matmul(z, h0T[:, 1, i * P:(i + 1) * P], Wh[:, :], start=True, stop=False)
                    last = nc.tensor.matmul(z, onesf[0:1, :], brow[0:1, 1, :], start=False, stop=True)
                last.then_inc(S["prod_done"], 1)

            pe.wait_ge(S["agg_done"], T)
            pe.wait_ge(S["dup_copied"], G)
            for i in range(NCH + 7):
                if i < NCH:
                    wait(pe, S["h0T_copied"], i)
                    transposes(i, 0, "h0T_done")
                    layer0_products(i)
                if 0 <= i - 5 < NCH:
                    pe.wait_ge(S["h1a_ready"], i - 5 + 1)
                    wait(pe, S["h1T_copied"], i - 5)
                    transposes(i - 5, 1, "h1T_done")
                if 0 <= i - 6 < NCH:
                    layer1_product(i - 6)

            pe.wait_ge(S["parts_ready"], NCH + 1)
            off_regs = [pe.alloc_register(f"off{j}") for j in range(J)]

            def attr_T(g, k):
                if not isinstance(g, int) or g <= FULL_G:
                    pe.wait_ge(S_attr[k], landed(g, k) + (16 if isinstance(g, int) and g == FULL_G else 0))
                wait(pe, S["attrT_ready"], g)
                for q in range(2):
                    last = nc.tensor.transpose(pTP[:, q, :], attr[:, k, q * 2 * R:(q + 1) * 2 * R], ident[:, :])
                last.then_inc(S["tp_done"], 1)

            def hidden(g, k):
                pe.wait_ge(S["attrT_ready"], g + 1)
                wait(pe, S["relu_done"], g)
                for h in range(2):
                    last = nc.tensor.matmul(pHID[:, h, :].rearrange("p (q e) -> p q e", q=2), W1s[h * R:(h + 1) * R, :],
                                            attrT[h * R:(h + 1) * R, k % 2, :, :], start=True, stop=True)
                last.then_inc(S["hid_done"], 1)

            def weights(g, k):
                pe.wait_ge(S["relu_done"], g + 1)
                wait(pe, S["msg_done"], g - 1)
                nc.tensor.matmul(pW[:, k % 2, :].rearrange("p (j c) -> p j c", j=J), onesb[0:3, :],
                                 b2p[:, :].unsqueeze(1).to_broadcast([3, J, C]), start=True, stop=False)
                for j in range(J):
                    last = nc.tensor.matmul(pW[:, k % 2, j * C:(j + 1) * C], hidT[:, k % 2, j % 2, j // 2, :], W2s[:, :],
                                            start=False, stop=(j == J - 1))
                last.then_inc(S["w_done"], 1)

            def node_rows(g, k):
                pe.load(off_regs, off_i[0:1, ds(g * J, J)])
                pe.wait_ge(S["oht_ready"], g + 1)
                wait(pe, S["hgc_done"], g)
                for j in range(J):
                    at = pe.snap(off_regs[j], min_val=0, max_val=(NB - 1) * 3 * C)
                    for n in range(6):
                        w, a = divmod(n, 3)
                        last = nc.tensor.matmul(pHG[:, j * C:(j + 1) * C], oht[:, k % 2, w, j * P:(j + 1) * P],
                                                h1p[:, ds(at + n * C, C)], start=(n == 0), stop=(n == 5))
                last.then_inc(S["hg_done"], 1)

            def equal_sums(g, k):
                pe.wait_ge(S["msg_done"], g + 1)
                pe.wait_ge(S["eqm_ready"], g + 1)
                wait(pe, S["out_ready"], g - 1)
                for j in range(J):
                    last = nc.tensor.matmul(pDD[:, k % 2, j * C:(j + 1) * C], eqm[:, k % 2, j, :], msg[:, k % 2, j * C:(j + 1) * C],
                                            start=True, stop=True)
                last.then_inc(S["dd_done"], 1)

            attr_T(0, 0)
            attr_T(1, 1)
            hidden(0, 0)

            def layer1(s, k):
                known = isinstance(s, int)
                node_rows(s, k)
                weights(s, k)
                if not known or s + 1 < G:
                    hidden(s + 1, (k + 1) % U)
                if not known or s + 2 < G:
                    attr_T(s + 2, (k + 2) % U)
                if not known or s > 0:
                    equal_sums(s - 1, (k - 1) % U)

            steps(pe, layer1)
            equal_sums(G - 1, (G - 1) % U)

        @block.scalar
        def _(act):
            def squares(c, n, slot, lag):
                act.wait_ge(S["lnT"], n + 1)
                wait(act, S["lnT_copied"], n - lag)
                nc.scalar.activation(E1[:, slot, :], H[:, chunk(c), :].rearrange("p b c -> p (b c)"), ACT.Square).then_inc(S["sq_done"], 1)

            def deviations(c, n):
                act.wait_ge(S["lnT_copied"], n + 1)
                nc.scalar.activation(var[:, chunk(c)], var[:, chunk(c)], ACT.Sqrt, bias=epsc[:, :]).then_inc(S["std_ready"], 1)

            for c in range(NCH + 1):
                if c < NCH:
                    squares(c, c, c % 2, 1)
                if c:
                    deviations(c - 1, c - 1)

            act.wait_ge(S["consts"], 7)
            act.dma_start(acc_d[0][N:NP, :], zeros[0:NP - N, 0:C]).then_inc(S_zero, 16)
            act.dma_start(acc_d[0][NP:ACCR, :], zeros[:, 0:C]).then_inc(S_zero, 16)
            for n in range((NACC - 1) * ZPARTS):
                a, z = n // ZPARTS, n % ZPARTS
                act.wait_ge(S["sums_done"], 5 * n + 1)
                act.dma_start(acc_d[1 + a].rearrange("(p b) c -> p (b c)", p=P)[:, z * 5 * C:(z + 1) * 5 * C], zeros[:, :])\
                    .then_inc(S_zero, 16)

            hp = h1p.rearrange("p (b a c) -> p b a c", a=3, c=C)
            for i in range(NCH + 9):
                if i < NCH:
                    act.wait_ge(S["h0T_done"], i + 1)
                    wait(act, S["z_done"], i)
                    nc.scalar.activation(h0T[:, 0, :], psT[:, 0, 0:CW], ACT.Copy).then_inc(S["h0T_copied"], 1)
                if 0 <= (c := i - 1) < NCH:
                    act.wait_ge(S["zs_ready"], c + 1)
                    wait(act, S["sum_ready"], c)
                    nc.scalar.activation(E1[:, 0, :], H[:, chunk(c), :].rearrange("p b c -> p (b c)"), ACT.Exp).then_inc(S["exp_done"], 1)
                if 0 <= (c := i - 2) < NCH:
                    act.wait_ge(S["sum_ready"], c + 1)
                    nc.scalar.activation(zsum[:, chunk(c)], zsum[:, chunk(c)], ACT.Ln).then_inc(S["ln_done"], 1)
                if 0 <= (c := i - 3) < NCH:
                    squares(c, NCH + c, 1, 0)
                if 0 <= (c := i - 4) < NCH:
                    deviations(c, NCH + c)
                if 0 <= (c := i - 5) < NCH:
                    act.wait_ge(S["h1T_done"], c + 1)
                    wait(act, S["prod_done"], c)
                    nc.scalar.activation(h0T[:, 1, :], psT[:, 1, 0:CW], ACT.Copy).then_inc(S["h1T_copied"], 1)
                if 0 <= (c := i - 6) < NCH:
                    act.wait_ge(S["prod_done"], c + 1)
                    nc.scalar.activation(hp[:, chunk(c), 0, :], psZ1[:, 0:CW].rearrange("p (b c) -> p b c", c=C), ACT.Copy)\
                        .then_inc(S["part0_ready"], 1)
                if 0 <= (c := i - 7) < NCH:
                    act.wait_ge(S["rest_ready"], c + 1)
                    nc.scalar.activation(hp[:, chunk(c), 1, :], H[:, chunk(c), :], ACT.Copy).then_inc(S["part1_ready"], 1)

            def attrT_copy(g, k):
                act.wait_ge(S["tp_done"], g + 1)
                wait(act, S["hid_done"], g - 1)
                nc.scalar.activation(attrT[:, k % 2, :, :], pTP, ACT.Copy).then_inc(S["attrT_ready"], 1)

            def relu(g, k):
                act.wait_ge(S["hid_done"], g + 1)
                wait(act, S["w_done"], g - 1)
                nc.scalar.activation(hidT[:, k % 2, :, :, :].rearrange("p h q e -> p h (q e)"), pHID, ACT.Relu,
                                     bias=b1c[:, :]).then_inc(S["relu_done"], 1)

            def rows_copy(g, k):
                act.wait_ge(S["hg_done"], g + 1)
                wait(act, S["msg_done"], g - 1)
                nc.scalar.activation(hgs[:, k % 2, :], pHG, ACT.Copy).then_inc(S["hgc_done"], 1)

            attrT_copy(0, 0)
            attrT_copy(1, 1)
            relu(0, 0)

            def layer1(s, k):
                known = isinstance(s, int)
                rows_copy(s, k)
                if not known or s + 1 < G:
                    relu(s + 1, (k + 1) % U)
                if not known or s + 2 < G:
                    attrT_copy(s + 2, (k + 2) % U)

            steps(act, layer1)


_INS = ["x", "src", "dst", "edge_attr_64", "L0_gnn_W_l", "L0_gnn_W_r", "L0_gnn_b", "L1_gnn_W1", "L1_gnn_b1",
        "L1_gnn_W2", "L1_gnn_b2", "L1_gnn_Wl", "L1_gnn_bl"]
_OUTS = [((6250, 128), "float32")]


def kernel(**inputs):
    import numpy as _np
    import concourse.bacc as _bacc
    from concourse import mybir as _mybir
    from concourse.bass_utils import run_bass_kernel_spmd as _run

    nc = _bacc.Bacc("TRN2", target_bir_lowering=False, num_devices=1)
    arrays, args = {}, []
    for name in _INS:
        a = _np.ascontiguousarray(inputs[name])
        arrays[f"in_{name}_dram"] = a
        args.append(nc.dram_tensor(f"in_{name}_dram", a.shape, _mybir.dt.from_np(a.dtype), kind="ExternalInput").ap())
    for i, (shape, dtype) in enumerate(_OUTS):
        dt = _mybir.dt.from_np(_np.dtype(dtype))
        args.append(nc.dram_tensor(f"out_{i}_dram", shape, dt, kind="ExternalOutput").ap())
    gnn_program(nc, *args)
    r = _run(nc, [arrays], core_ids=[0])
    got = tuple(r.results[0][f"out_{i}_dram"] for i in range(len(_OUTS)))
    return got[0]
```
